# Optimizing a Trainium2 kernel written in Bass

```python
import numpy as np
import jax
import jax.numpy as jnp

def _softmax(x, axis=-1):
    return jax.nn.softmax(x, axis=axis)

def _gelu(x):
    return jax.nn.gelu(x, approximate=True)

def _silu(x):
    return jax.nn.silu(x)

def _sigmoid(x):
    return jax.nn.sigmoid(x)

def _layernorm(x, axis=-1, eps=1e-05):
    m = jnp.mean(x, axis=axis, keepdims=True)
    v = jnp.var(x, axis=axis, keepdims=True)
    return (x - m) / jnp.sqrt(v + eps)

def _scatter_add(tgt, idx, src, axis=0):
    return tgt.at[idx].add(src)

def _segment_sum(src, seg, n):
    return jax.ops.segment_sum(src, seg, n)
kernel_name = 'mk_lm_tower_d2_tok_ids256_r4_24e6df'

def setup_inputs(seed: int=0):
    np.random.seed(seed)
    _w = jnp.asarray

    def _rec_inputs():
        import jax
        import jax.numpy as jnp
        _rk = jax.random.key(seed)
        x = jax.random.randint(jax.random.fold_in(_rk, 1), (4, 1024), 0, 4360, jnp.int32)
        return x
    x = _rec_inputs()

    def _L0_tok_setup():
        import jax, jax.numpy as jnp
        import numpy as np
        VOCAB = 4360
        PROJ = 64
        PAD_IDX = 0
        key = jax.random.key(seed)
        k1, k2 = jax.random.split(key)
        x = jax.random.randint(k1, (64, 512), 0, VOCAB, dtype=jnp.int64)
        W = jax.random.normal(k2, (PROJ, VOCAB), dtype=jnp.float32) * 0.02
        return {'x': x, 'W': W}
    _L0_tok_all = _L0_tok_setup()
    _L0_tok_in = {k: v for k, v in _L0_tok_all.items() if k in ('W',)}
    del _L0_tok_all

    def _L0_attn_setup():
        import jax, jax.numpy as jnp
        import numpy as np
        B, N, E, H = (4, 1024, 64, 8)
        EXP = 3
        D1 = EXP * E // H * H
        HD = D1 // H
        RPE = int(min(E / 8, 32))
        LAYERS = 3
        EPS = 1e-08

        def _srms(x, d):
            rms = jnp.linalg.norm(x, axis=-1, keepdims=True) * d ** (-0.5)
            return x / (rms + EPS)

        def _rpe(idx, pos_w, pos_b, rpe_lw, rpe_lb, out_w, out_b):
            h = idx @ pos_w.T + pos_b
            for i in range(LAYERS):
                h = jax.nn.relu(_srms(h, RPE)) @ rpe_lw[i].T + rpe_lb[i]
            return jax.nn.relu(_srms(h, RPE)) @ out_w.T + out_b
        key = jax.random.key(seed)
        ks = jax.random.split(key, 9)
        s = lambda k, shape, fan: jax.random.normal(k, shape, jnp.float32) * fan ** (-0.5)
        return {'x': jax.random.normal(ks[0], (B, N, E), jnp.float32), 'u_w': s(ks[1], (D1, E), E), 'u_b': jnp.zeros((D1,), jnp.float32), 'v_w': s(ks[2], (D1, E), E), 'v_b': jnp.zeros((D1,), jnp.float32), 'o_w': s(ks[3], (E, D1), D1), 'o_b': jnp.zeros((E,), jnp.float32), 't_w': s(ks[4], (E, E), E), 't_b': jnp.zeros((E,), jnp.float32), 'pos_w': s(ks[5], (RPE, 1), 1), 'pos_b': jnp.zeros((RPE,), jnp.float32), 'rpe_lw': s(ks[6], (LAYERS, RPE, RPE), RPE), 'rpe_lb': jnp.zeros((LAYERS, RPE), jnp.float32), 'out_w': s(ks[7], (H * HD, RPE), RPE), 'out_b': jnp.zeros((H * HD,), jnp.float32)}
    _L0_attn_all = _L0_attn_setup()
    _L0_attn_in = {k: v for k, v in _L0_attn_all.items() if k in ('u_w', 'u_b', 'v_w', 'v_b', 'o_w', 'o_b', 't_w', 't_b', 'pos_w', 'pos_b', 'rpe_lw', 'rpe_lb', 'out_w', 'out_b')}
    del _L0_attn_all

    def _L0_ffn_setup():
        import jax, jax.numpy as jnp
        import numpy as np
        DIM = 64
        HEADS = 8
        NUM_KEYS = 64
        NUM_KV = NUM_KEYS ** 2
        PK_TOPK = 16
        FINAL_TOPK = 16
        DIM_KEY = DIM // 2
        P = 2

        def _pk(x, Wq_pk, pk_keys):
            b, n, _ = x.shape
            q = (x @ Wq_pk).reshape(b, n, P, HEADS, DIM_KEY).transpose(2, 0, 1, 3, 4)
            sim = jnp.einsum('pbnhd,pkhd->pbnhk', q, pk_keys)
            scores, idx = jax.lax.top_k(sim, PK_TOPK)
            idx0 = idx[0]
            idx1 = idx[1] * NUM_KEYS
            index = (idx0[..., :, None] + idx1[..., None, :]).reshape(b, n, HEADS, PK_TOPK * PK_TOPK)
            score = (scores[0][..., :, None] + scores[1][..., None, :]).reshape(b, n, HEADS, PK_TOPK * PK_TOPK)
            final_scores, pk_idx = jax.lax.top_k(score, FINAL_TOPK)
            final_indices = jnp.take_along_axis(index, pk_idx, axis=-1)
            final_scores = jax.nn.softmax(final_scores, axis=-1)
            return (final_scores, final_indices)
        key = jax.random.key(seed)
        ks = jax.random.split(key, 7)
        b, n = (2, 256)
        std = 0.02
        x = jax.random.normal(ks[0], (b, n, DIM), dtype=jnp.float32)
        Wq_pk = jax.random.normal(ks[1], (DIM, P * HEADS * DIM_KEY), dtype=jnp.float32) * std
        pk_keys = jax.random.normal(ks[2], (P, NUM_KEYS, HEADS, DIM_KEY), dtype=jnp.float32) * std
        Wq = jax.random.normal(ks[3], (DIM, HEADS * DIM), dtype=jnp.float32) * std
        keys_table = jax.random.normal(ks[4], (NUM_KV * HEADS, DIM), dtype=jnp.float32) * std
        values_table = jax.random.normal(ks[5], (NUM_KV * HEADS, DIM), dtype=jnp.float32) * std
        Wo = jax.random.normal(ks[6], (DIM * HEADS, DIM), dtype=jnp.float32) * std
        return {'x': x, 'Wq_pk': Wq_pk, 'pk_keys': pk_keys, 'Wq': Wq, 'keys_table': keys_table, 'values_table': values_table, 'Wo': Wo}
    _L0_ffn_all = _L0_ffn_setup()
    _L0_ffn_in = {k: v for k, v in _L0_ffn_all.items() if k in ('Wq_pk', 'pk_keys', 'Wq', 'keys_table', 'values_table', 'Wo')}
    del _L0_ffn_all

    def _L1_attn_setup():
        import jax, jax.numpy as jnp
        import numpy as np
        key = jax.random.key(seed)
        k1, k2, k3 = jax.random.split(key, 3)
        d = 64
        x = jax.random.normal(k1, (8, 512, d), dtype=jnp.float32)
        Wq = jax.random.normal(k2, (d, d), dtype=jnp.float32) * d ** (-0.5)
        Wk = jax.random.normal(k3, (d, d), dtype=jnp.float32) * d ** (-0.5)
        return {'x': x, 'Wq': Wq, 'Wk': Wk}
    _L1_attn_all = _L1_attn_setup()
    _L1_attn_in = {k: v for k, v in _L1_attn_all.items() if k in ('Wq', 'Wk')}
    del _L1_attn_all

    def _L1_ffn_setup():
        import jax, jax.numpy as jnp
        import numpy as np
        NUM_EXPERTS = 8
        TOP_K = 2
        B, S, D = (8, 2048, 64)

        def _moe(tokens, router_w, w1, b1, w2, b2):
            N = tokens.shape[0]
            E = router_w.shape[0]
            logits = tokens.astype(jnp.float32) @ router_w.astype(jnp.float32).T
            probs = jax.nn.softmax(logits, axis=-1)
            rw, re = jax.lax.top_k(probs, TOP_K)
            if TOP_K > 1:
                rw = rw / jnp.maximum(rw.sum(-1, keepdims=True), 1e-12)
            rw = rw.astype(tokens.dtype)
            combine = jnp.zeros((N, E), tokens.dtype).at[jnp.arange(N)[:, None], re].set(rw)
            out = tokens
            for e in range(E):
                h = jax.nn.gelu(tokens @ w1[e] + b1[e], approximate=False)
                y = h @ w2[e] + b2[e]
                out = out + combine[:, e:e + 1] * y
            return out
        key = jax.random.key(seed)
        ks = jax.random.split(key, 4)
        scale = 1.0 / np.sqrt(D).astype(np.float32)
        return {'input_embeddings': jax.random.normal(ks[0], (B, S, D), jnp.float32), 'router_w': jax.random.normal(ks[1], (NUM_EXPERTS, D), jnp.float32) * scale, 'w1': jax.random.normal(ks[2], (NUM_EXPERTS, D, D), jnp.float32) * scale, 'b1': jnp.zeros((NUM_EXPERTS, D), jnp.float32), 'w2': jax.random.normal(ks[3], (NUM_EXPERTS, D, D), jnp.float32) * scale, 'b2': jnp.zeros((NUM_EXPERTS, D), jnp.float32)}
    _L1_ffn_all = _L1_ffn_setup()
    _L1_ffn_in = {k: v for k, v in _L1_ffn_all.items() if k in ('router_w', 'w1', 'b1', 'w2', 'b2')}
    del _L1_ffn_all
    return {'x': x, 'L0_tok_W': _L0_tok_in['W'], 'L0_attn_u_w': _L0_attn_in['u_w'], 'L0_attn_u_b': _L0_attn_in['u_b'], 'L0_attn_v_w': _L0_attn_in['v_w'], 'L0_attn_v_b': _L0_attn_in['v_b'], 'L0_attn_o_w': _L0_attn_in['o_w'], 'L0_attn_o_b': _L0_attn_in['o_b'], 'L0_attn_t_w': _L0_attn_in['t_w'], 'L0_attn_t_b': _L0_attn_in['t_b'], 'L0_attn_pos_w': _L0_attn_in['pos_w'], 'L0_attn_pos_b': _L0_attn_in['pos_b'], 'L0_attn_rpe_lw': _L0_attn_in['rpe_lw'], 'L0_attn_rpe_lb': _L0_attn_in['rpe_lb'], 'L0_attn_out_w': _L0_attn_in['out_w'], 'L0_attn_out_b': _L0_attn_in['out_b'], 'L0_ffn_Wq_pk': _L0_ffn_in['Wq_pk'], 'L0_ffn_pk_keys': _L0_ffn_in['pk_keys'], 'L0_ffn_Wq': _L0_ffn_in['Wq'], 'L0_ffn_keys_table': _L0_ffn_in['keys_table'], 'L0_ffn_values_table': _L0_ffn_in['values_table'], 'L0_ffn_Wo': _L0_ffn_in['Wo'], 'L1_attn_Wq': _L1_attn_in['Wq'], 'L1_attn_Wk': _L1_attn_in['Wk'], 'L1_ffn_router_w': _L1_ffn_in['router_w'], 'L1_ffn_w1': _L1_ffn_in['w1'], 'L1_ffn_b1': _L1_ffn_in['b1'], 'L1_ffn_w2': _L1_ffn_in['w2'], 'L1_ffn_b2': _L1_ffn_in['b2']}

def reference(x, L0_tok_W, L0_attn_u_w, L0_attn_u_b, L0_attn_v_w, L0_attn_v_b, L0_attn_o_w, L0_attn_o_b, L0_attn_t_w, L0_attn_t_b, L0_attn_pos_w, L0_attn_pos_b, L0_attn_rpe_lw, L0_attn_rpe_lb, L0_attn_out_w, L0_attn_out_b, L0_ffn_Wq_pk, L0_ffn_pk_keys, L0_ffn_Wq, L0_ffn_keys_table, L0_ffn_values_table, L0_ffn_Wo, L1_attn_Wq, L1_attn_Wk, L1_ffn_router_w, L1_ffn_w1, L1_ffn_b1, L1_ffn_w2, L1_ffn_b2):
    import jax
    import jax.numpy as jnp

    def _L0_tok_ref(x, W):
        import jax, jax.numpy as jnp
        import numpy as np
        VOCAB = 4360
        PROJ = 64
        PAD_IDX = 0
        out = jnp.take(W.T, x, axis=0)
        mask = (x != PAD_IDX)[..., None]
        return jnp.where(mask, out, jnp.zeros((), dtype=out.dtype))

    def _L0_attn_ref(x, u_w, u_b, v_w, v_b, o_w, o_b, t_w, t_b, pos_w, pos_b, rpe_lw, rpe_lb, out_w, out_b):
        import jax, jax.numpy as jnp
        import numpy as np
        B, N, E, H = (4, 1024, 64, 8)
        EXP = 3
        D1 = EXP * E // H * H
        HD = D1 // H
        RPE = int(min(E / 8, 32))
        LAYERS = 3
        EPS = 1e-08

        def _srms(x, d):
            rms = jnp.linalg.norm(x, axis=-1, keepdims=True) * d ** (-0.5)
            return x / (rms + EPS)

        def _rpe(idx, pos_w, pos_b, rpe_lw, rpe_lb, out_w, out_b):
            h = idx @ pos_w.T + pos_b
            for i in range(LAYERS):
                h = jax.nn.relu(_srms(h, RPE)) @ rpe_lw[i].T + rpe_lb[i]
            return jax.nn.relu(_srms(h, RPE)) @ out_w.T + out_b
        b, n, _ = x.shape
        u = jax.nn.silu(x @ u_w.T + u_b)
        v = jax.nn.silu(x @ v_w.T + v_b)
        v = v.reshape(b, n, H, HD).transpose(0, 2, 1, 3)
        pos_idx = jnp.arange(1, n, dtype=jnp.float32)
        idx = jnp.concatenate([jnp.zeros((1,), jnp.float32), pos_idx, jnp.zeros((1,), jnp.float32), -pos_idx[::-1]])[:, None]
        a = _rpe(idx, pos_w, pos_b, rpe_lw, rpe_lb, out_w, out_b)
        a = a.reshape(2 * n, H, HD).transpose(1, 0, 2)
        yf = jnp.fft.rfft(v, 2 * n, axis=-2)
        af = jnp.fft.rfft(a, 2 * n, axis=-2)[None]
        out = jnp.fft.irfft(af * yf, 2 * n, axis=-2)[:, :, :n, :]
        out = out.transpose(0, 2, 1, 3).reshape(b, n, D1)
        out = u * out @ o_w.T + o_b
        x_r = jax.nn.silu(_srms((x - out) @ t_w.T + t_b, D1))
        return x + x_r

    def _L0_ffn_ref(x, Wq_pk, pk_keys, Wq, keys_table, values_table, Wo):
        import jax, jax.numpy as jnp
        import numpy as np
        DIM = 64
        HEADS = 8
        NUM_KEYS = 64
        NUM_KV = NUM_KEYS ** 2
        PK_TOPK = 16
        FINAL_TOPK = 16
        DIM_KEY = DIM // 2
        P = 2

        def _pk(x, Wq_pk, pk_keys):
            b, n, _ = x.shape
            q = (x @ Wq_pk).reshape(b, n, P, HEADS, DIM_KEY).transpose(2, 0, 1, 3, 4)
            sim = jnp.einsum('pbnhd,pkhd->pbnhk', q, pk_keys)
            scores, idx = jax.lax.top_k(sim, PK_TOPK)
            idx0 = idx[0]
            idx1 = idx[1] * NUM_KEYS
            index = (idx0[..., :, None] + idx1[..., None, :]).reshape(b, n, HEADS, PK_TOPK * PK_TOPK)
            score = (scores[0][..., :, None] + scores[1][..., None, :]).reshape(b, n, HEADS, PK_TOPK * PK_TOPK)
            final_scores, pk_idx = jax.lax.top_k(score, FINAL_TOPK)
            final_indices = jnp.take_along_axis(index, pk_idx, axis=-1)
            final_scores = jax.nn.softmax(final_scores, axis=-1)
            return (final_scores, final_indices)
        b, n, d = x.shape
        q = (x @ Wq).reshape(b, n, HEADS, DIM) * DIM ** (-0.5)
        kv_scores, indices = _pk(x, Wq_pk, pk_keys)
        offsets = jnp.arange(HEADS, dtype=indices.dtype) * NUM_KV
        ind = indices + offsets[None, None, :, None]
        k = jnp.einsum('bnhk,bnhkd->bnhd', kv_scores, keys_table[ind])
        v = jnp.einsum('bnhk,bnhkd->bnhd', kv_scores, values_table[ind])
        sim = jnp.einsum('bihd,bjhd->bhij', q, k)
        neg = -jnp.finfo(sim.dtype).max
        causal = jnp.tril(jnp.ones((n, n), dtype=bool))
        sim = jnp.where(causal, sim, neg)
        attn = jax.nn.softmax(sim, axis=-1)
        out = jnp.einsum('bhij,bjhd->bhid', attn, v)
        out = out.transpose(0, 2, 1, 3).reshape(b, n, HEADS * DIM)
        return out @ Wo

    def _L1_attn_ref(x, Wq, Wk):
        import jax, jax.numpy as jnp
        import numpy as np
        d = x.shape[-1]
        scale = d ** (-0.5)
        q = jnp.einsum('bnd,ed->bne', x, Wq)
        k = jnp.einsum('bnd,ed->bne', x, Wk)
        sim = jnp.einsum('bid,bjd->bij', q, k) * scale
        attn = jax.nn.softmax(sim, axis=-1)
        out = jnp.einsum('bij,bjd->bid', attn, x)
        return out

    def _L1_ffn_ref(input_embeddings, router_w, w1, b1, w2, b2):
        import jax, jax.numpy as jnp
        import numpy as np
        NUM_EXPERTS = 8
        TOP_K = 2
        B, S, D = (8, 2048, 64)

        def _moe(tokens, router_w, w1, b1, w2, b2):
            N = tokens.shape[0]
            E = router_w.shape[0]
            logits = tokens.astype(jnp.float32) @ router_w.astype(jnp.float32).T
            probs = jax.nn.softmax(logits, axis=-1)
            rw, re = jax.lax.top_k(probs, TOP_K)
            if TOP_K > 1:
                rw = rw / jnp.maximum(rw.sum(-1, keepdims=True), 1e-12)
            rw = rw.astype(tokens.dtype)
            combine = jnp.zeros((N, E), tokens.dtype).at[jnp.arange(N)[:, None], re].set(rw)
            out = tokens
            for e in range(E):
                h = jax.nn.gelu(tokens @ w1[e] + b1[e], approximate=False)
                y = h @ w2[e] + b2[e]
                out = out + combine[:, e:e + 1] * y
            return out
        b, s, d = input_embeddings.shape
        tokens = input_embeddings.reshape(b * s, d)
        return _moe(tokens, router_w, w1, b1, w2, b2).reshape(b, s, d)
    h = _L0_tok_ref(x, L0_tok_W)
    h = h + _L0_attn_ref(_layernorm(h, axis=-1), L0_attn_u_w, L0_attn_u_b, L0_attn_v_w, L0_attn_v_b, L0_attn_o_w, L0_attn_o_b, L0_attn_t_w, L0_attn_t_b, L0_attn_pos_w, L0_attn_pos_b, L0_attn_rpe_lw, L0_attn_rpe_lb, L0_attn_out_w, L0_attn_out_b)
    h = h + _L0_ffn_ref(_layernorm(h, axis=-1), L0_ffn_Wq_pk, L0_ffn_pk_keys, L0_ffn_Wq, L0_ffn_keys_table, L0_ffn_values_table, L0_ffn_Wo)
    h = h + _L1_attn_ref(_layernorm(h, axis=-1), L1_attn_Wq, L1_attn_Wk)
    h = h + _L1_ffn_ref(_layernorm(h, axis=-1), L1_ffn_router_w, L1_ffn_w1, L1_ffn_b1, L1_ffn_w2, L1_ffn_b2)
    return h

_drawn_inputs = setup_inputs


def setup_inputs(seed=0):
    import zlib

    import numpy as np

    out = dict(_drawn_inputs(seed))
    spreads = {'L0_attn_u_b': (0.0, 0.1),
     'L0_attn_v_b': (0.0, 0.1),
     'L0_attn_o_b': (0.0, 2.0),
     'L0_attn_t_b': (0.0, 2.0),
     'L0_attn_pos_b': (0.0, 2.0),
     'L0_attn_rpe_lb': (0.0, 0.1),
     'L0_attn_out_b': (0.0, 0.1),
     'L1_ffn_b1': (0.0, 0.385),
     'L1_ffn_b2': (0.0, 0.1)}
    factors = {'L0_ffn_Wq_pk': 8.0,
     'L0_ffn_pk_keys': 8.0,
     'L0_ffn_Wq': 64.0,
     'L0_ffn_keys_table': 64.0,
     'L0_ffn_values_table': 8.0,
     'L0_ffn_Wo': 8.0}
    for name, (base, spread) in spreads.items():
        noise = np.random.default_rng([zlib.crc32(name.encode()), seed]).standard_normal(out[name].shape)
        drawn = base * np.exp(spread * noise) if base else spread * noise
        out[name] = jnp.asarray(drawn.astype(out[name].dtype))
    for name, factor in factors.items():
        out[name] = (out[name] * factor).astype(out[name].dtype)
    return out
```

```python
from contextlib import ExitStack

import numpy as np

import concourse.bass as bass
from concourse import mybir

F32 = mybir.dt.float32
BF16 = mybir.dt.bfloat16
I32 = mybir.dt.int32
U32 = mybir.dt.uint32
ALU = mybir.AluOpType
ACT = mybir.ActivationFunctionType
AX = mybir.AxisListType.X

P = 128
B, N, D = 4, 1024, 64
NB = N // P
T = B * N
TB = T // P
D1 = 192
RPE, LAYERS = 8, 3
FB = N // P
H = 8
DK = 32
NK = 64
TOPK = 16
RECTS = [(0, 1, 16), (1, 1, 8), (2, 2, 5), (4, 4, 3), (8, 8, 1)]
CAND = sum(na * nb for _, na, nb in RECTS)
E = 8
VOCAB = 4360
LN_EPS = 1e-5
RMS_EPS = 1e-8
LOWEST = -3.0e38
MASKED = -1.0e30


def tower_constants():
    j = np.arange(N)
    k = np.arange(N)
    turn = 2 * np.pi * ((j[:, None] * k[None, :]) % (2 * N)) / (2 * N)
    re, im = np.cos(turn), -np.sin(turn)
    im[:, 0] = (-1.0) ** j
    fwd = np.stack([re, im], 0).reshape(2, NB, P, FB, P)
    dft = np.ascontiguousarray(fwd.transpose(3, 2, 1, 0, 4).reshape(FB * P, NB * 2 * P)).astype(np.float32)
    gain = np.full(N, 2.0 / (2 * N))
    gain[0] = 1.0 / (2 * N)
    ire, iim = re * gain, im * gain
    inv = np.stack([ire, iim], 0).reshape(2, NB, P, FB, P)
    idft = np.ascontiguousarray(inv.transpose(1, 4, 3, 0, 2).reshape(NB * P, FB * 2 * P)).astype(np.float32)
    sign = np.ones((16, FB, 2, P), np.float32)
    odd = (k.reshape(FB, P) % 2) == 1
    sign[8:] = np.where(odd, -1.0, 1.0)[None, :, None, :]
    keep = np.ones((17, FB, P), np.float32)
    keep[:, 0, 0] = 0.0
    offset = np.zeros((1, FB, 2, P), np.float32)
    offset[0, 0, 0, 0] = 2 * N
    pos = np.concatenate([[0.0], np.arange(1, N), [0.0], -np.arange(1, N)[::-1]]).astype(np.float32)
    causal = np.where(np.arange(P)[None, :] > np.arange(P)[:, None], MASKED, 0.0).astype(np.float32)
    return {
        "c_ident": np.eye(P, dtype=np.float32),
        "c_dft": dft,
        "c_idft": idft,
        "c_sign": sign.reshape(16, FB * 2 * P),
        "c_keep": keep.reshape(17, FB * P),
        "c_offset": offset.reshape(1, FB * 2 * P),
        "c_pos": np.ascontiguousarray(pos.reshape(2 * NB, P).T),
        "c_causal": causal,
        "c_causalT": np.ascontiguousarray(causal.T),
        "c_rank": np.tile(np.arange(CAND, dtype=np.float32), (P, 1)),
        "c_head": np.tile(np.repeat(np.arange(H, dtype=np.float32) * NK * NK, TOPK), (P, 1)),
        "c_expert": np.tile(np.arange(E, dtype=np.float32), (P, 1)),
    }


class Chain:

    def __init__(self, engine, semaphore):
        self.engine, self.semaphore, self.count = engine, semaphore, 0

    def mark(self, instruction):
        self.count += 1
        return instruction.then_inc(self.semaphore, 1)

    def wait(self):
        self.engine.wait_ge(self.semaphore, self.count)

    def link(self, instruction):
        self.mark(instruction)
        self.wait()

    def clear(self):
        self.wait()
        self.engine.sem_clear(self.semaphore)
        self.count = 0


def bc(ap, axis, n):
    shape = list(ap.shape)
    return ap.unsqueeze(axis).broadcast_to(shape[:axis] + [n] + shape[axis:])




class Mem:

    def __init__(self, nc, ctx, stage):
        self.nc, self.ctx, self.stage = nc, ctx, stage

    def sb(self, name, shape, dt=F32):
        return self.ctx.enter_context(self.nc.sbuf_tensor(f"{self.stage}_{name}", shape, dt))

    def ps(self, name, shape, dt=F32):
        return self.ctx.enter_context(self.nc.psum_tensor(f"{self.stage}_{name}", shape, dt))

    def sem(self, name):
        return self.ctx.enter_context(self.nc.semaphore(f"{self.stage}_{name}"))


def layernorm_a(dve, chain, x, xc, sq, stat):
    chain.link(dve.tensor_reduce(stat[:, 0, :], x, AX, ALU.add))
    chain.link(dve.tensor_scalar(stat[:, 1, :], stat[:, 0, :], -1.0 / D, None, ALU.mult))
    chain.link(dve.tensor_tensor(xc, x, bc(stat[:, 1, :], 2, D), ALU.add))
    chain.link(dve.tensor_tensor(sq, xc, xc, ALU.mult))
    chain.link(dve.tensor_reduce(stat[:, 2, :], sq, AX, ALU.add))
    chain.link(dve.tensor_scalar(stat[:, 2, :], stat[:, 2, :], 1.0 / D, LN_EPS, ALU.mult, ALU.add))


def layernorm_b(dve, chain, xn, xc, stat):
    chain.link(dve.reciprocal(stat[:, 1, :], stat[:, 3, :]))
    return dve.tensor_tensor(xn, xc, bc(stat[:, 1, :], 2, D), ALU.mult)


def flip_rows(pe, out, x, ident):
    pe.matmul(out[0:D, 0:P], x[:, 0, 0:D], ident[:, :], start=True, stop=True)
    for t in range(1, NB):
        last = pe.transpose(out[0:D, t * P:(t + 1) * P], x[:, t, 0:D], ident[:, :])
    return last


def embed_stage(nc, a, st):
    with ExitStack() as ctx:
        m = Mem(nc, ctx, "em")
        ids = m.sb("ids", [P, TB], I32)
        not_pad = m.sb("not_pad", [P, TB])
        ident = m.sb("ident", [P, P])
        uv_w = m.sb("uv_w", [D + 1, 2 * D1])
        rpe_w = m.sb("rpe_w", [P, 2 * RPE + LAYERS * (RPE * RPE + RPE)])
        pos = m.sb("pos", [P, 2 * NB])
        xc = m.sb("xc", [P, NB, D])
        sq = m.sb("sq", [P, NB, D])
        xn = m.sb("xn", [P, NB, D])
        stat = m.sb("stat", [P, 4, NB])
        xnT = m.sb("xnT", [D + 1, N])
        rh = m.sb("rh", [P, 2 * NB, RPE])
        rr = m.sb("rr", [P, 2 * NB, RPE])
        rprod = m.sb("rprod", [P, 2 * NB, RPE, RPE])
        rstat = m.sb("rstat", [P, 4, 2 * NB])
        xnT_ps = m.ps("xnT_ps", [D, N])
        uv_ps = m.ps("uv_ps", [P, 2, 512])

        loaded = m.sem("loaded")
        ids_in = m.sem("ids_in")
        embedded = m.sem("embedded")
        dve_steps = m.sem("dve_steps")
        act_steps = m.sem("act_steps")
        rpe_square = m.sem("rpe_square")
        rpe_root = m.sem("rpe_root")
        ln_var = m.sem("ln_var")
        ln_std = m.sem("ln_std")
        xn_ready = m.sem("xn_ready")
        xnT_ready = m.sem("xnT_ready")
        xnT_copied = m.sem("xnT_copied")
        uv_ready = m.sem("uv_ready")
        uv_taken = m.sem("uv_taken")
        ones_set = m.sem("ones_set")
        block = ctx.enter_context(nc.Block())

        @block.sync
        def _(sp):
            for semaphore in (xnT_ready, uv_ready, xnT_copied, uv_taken):
                sp.sem_inc(semaphore, 1)
            sp.dma_start(ids[:, :], a["ids"]).then_inc(ids_in, 16)
            sp.dma_start(rpe_w[:, :], a["rpe_w"].partition_broadcast(P)).then_inc(loaded, 16)
            sp.dma_start(pos[:, :], a["c_pos"]).then_inc(loaded, 16)
            sp.dma_start(ident[:, :], a["c_ident"]).then_inc(loaded, 16)
            sp.dma_start(uv_w[:, :], a["uv_w"]).then_inc(loaded, 16)

        @block.gpsimd
        def _(pool):
            pool.wait_ge(ids_in, 16)
            for t in range(TB):
                pool.indirect_dma_start(
                    st["h"][:, t, :], None, a["tok_W"],
                    bass.IndirectOffsetOnAxis(ids[:, t:t + 1].bitcast(U32), 0)).then_inc(embedded, 16)

        @block.vector
        def _(dve):
            chain = Chain(dve, dve_steps)
            dve.memset(xnT[D:D + 1, :], 1.0).then_inc(ones_set, 1)
            dve.wait_ge(ids_in, 16)
            chain.link(dve.tensor_scalar(not_pad[:, :], ids[:, :], 0.0, None, ALU.not_equal))
            dve.wait_ge(loaded, 64)
            w = rpe_w[:, :]
            chain.link(dve.tensor_tensor(rh[:, :, :], bc(pos[:, :], 2, RPE), bc(w[:, 0:RPE], 1, 2 * NB), ALU.mult))
            chain.link(dve.tensor_tensor(rh[:, :, :], rh[:, :, :], bc(w[:, RPE:2 * RPE], 1, 2 * NB), ALU.add))
            for layer in range(LAYERS + 1):
                chain.link(dve.tensor_tensor(rr[:, :, :], rh[:, :, :], rh[:, :, :], ALU.mult))
                chain.link(dve.tensor_reduce(rstat[:, 0, :], rr[:, :, :], AX, ALU.add))
                dve.tensor_scalar(rstat[:, 1, :], rstat[:, 0, :], 1.0 / RPE, None, ALU.mult).then_inc(rpe_square, 1)
                dve.wait_ge(rpe_root, layer + 1)
                chain.link(dve.tensor_scalar(rstat[:, 3, :], rstat[:, 2, :], RMS_EPS, None, ALU.add))
                chain.link(dve.reciprocal(rstat[:, 0, :], rstat[:, 3, :]))
                chain.link(dve.tensor_tensor(rr[:, :, :], rh[:, :, :], bc(rstat[:, 0, :], 2, RPE), ALU.mult))
                if layer == LAYERS:
                    out = st["rpe"][:, :, :, :].rearrange("p t s c -> p s t c")
                    src = rr[:, :, :].rearrange("p (s t) c -> p s t c", s=2)
                    chain.link(dve.tensor_scalar(out[:, 0], src[:, 0], 0.0, None, ALU.max))
                    chain.link(dve.tensor_scalar(out[:, 1], src[:, 1], 0.0, None, ALU.max))
                    continue
                chain.link(dve.tensor_scalar(rr[:, :, :], rr[:, :, :], 0.0, None, ALU.max))
                at = 2 * RPE + layer * RPE * RPE
                wl = w[:, at:at + RPE * RPE].rearrange("p (o c) -> p o c", c=RPE)
                for o in range(RPE):
                    chain.mark(dve.tensor_tensor(rprod[:, :, o, :], rr[:, :, :], bc(wl[:, o, :], 1, 2 * NB), ALU.mult))
                chain.wait()
                chain.link(dve.tensor_reduce(rh[:, :, :], rprod[:, :, :, :], AX, ALU.add))
                at = 2 * RPE + LAYERS * RPE * RPE + layer * RPE
                chain.link(dve.tensor_tensor(rh[:, :, :], rh[:, :, :], bc(w[:, at:at + RPE], 1, 2 * NB), ALU.add))
            dve.wait_ge(embedded, 16 * TB)
            chain.link(dve.tensor_tensor(st["h"][:, :, :], st["h"][:, :, :], bc(not_pad[:, :], 2, D), ALU.mult))
            chain.clear()
            with dve.Fori(0, B) as b:
                layernorm_a(dve, chain, st["h"][:, bass.ds(b * NB, NB), :], xc[:, :, :], sq[:, :, :], stat)
                chain.link(dve.tensor_copy(stat[:, 1, :], stat[:, 2, :]))
                dve.tensor_copy(stat[:, 0, :], stat[:, 2, :]).then_inc(ln_var, 1)
                dve.wait_ge(ln_std, b + 1)
                chain.link(dve.reciprocal(stat[:, 1, :], stat[:, 3, :]))
                dve.wait_ge(xnT_ready, b + 1)
                chain.link(dve.tensor_tensor(xn[:, :, :], xc[:, :, :], bc(stat[:, 1, :], 2, D), ALU.mult))
                dve.tensor_copy(st["xn"][:, bass.ds(b * NB, NB), :], xn[:, :, :]).then_inc(xn_ready, 1)
                chain.clear()

        @block.scalar
        def _(act):
            chain = Chain(act, act_steps)
            for layer in range(LAYERS + 1):
                act.wait_ge(rpe_square, layer + 1)
                act.activation(rstat[:, 2, :], rstat[:, 1, :], ACT.Sqrt).then_inc(rpe_root, 1)
            with act.Fori(0, B) as b:
                act.wait_ge(ln_var, b + 1)
                act.activation(stat[:, 3, :], stat[:, 0, :], ACT.Sqrt).then_inc(ln_std, 1)
                act.wait_ge(xnT_ready, b + 2)
                act.wait_ge(uv_ready, b * NB + 1)
                act.activation(xnT[0:D, :], xnT_ps[:, :], ACT.Copy).then_inc(xnT_copied, 1)
                chain.link(act.activation(st["xnT"][:, bass.ds(b * N, N)], xnT_ps[:, :], ACT.Copy))
                for t in range(NB):
                    act.wait_ge(uv_ready, b * NB + t + 2)
                    act.activation(st["u"][:, bass.ds(b * NB + t, 1), :], uv_ps[:, t % 2, 0:D1], ACT.Silu)\
                       .then_inc(act_steps, 1)
                    act.activation(st["v"][:, t, bass.ds(b, 1), :], uv_ps[:, t % 2, D1:2 * D1], ACT.Silu)\
                       .then_inc(uv_taken, 1)
                chain.count += NB
                chain.clear()

        @block.tensor
        def _(pe):
            pe.wait_ge(loaded, 64)
            pe.wait_ge(ones_set, 1)
            with pe.Fori(0, B) as b:
                pe.wait_ge(xn_ready, b + 1)
                pe.wait_ge(xnT_copied, b + 1)
                pe.wait_ge(uv_taken, b * NB + 1)
                flip_rows(pe, xnT_ps, xn, ident).then_inc(xnT_ready, 1)
                pe.wait_ge(xnT_copied, b + 2)
                for t in range(NB):
                    if t >= 2:
                        pe.wait_ge(uv_taken, b * NB + t)
                    pe.matmul(uv_ps[:, t % 2, 0:2 * D1], xnT[:, t * P:(t + 1) * P], uv_w[:, :],
                              start=True, stop=True).then_inc(uv_ready, 1)


def conv_stage(nc, a, st):
    HALF = B * D1 // 2
    with ExitStack() as ctx:
        m = Mem(nc, ctx, "cv")
        sign = m.sb("sign", [16, FB * 2 * P])
        keep = m.sb("keep", [17, FB * P])
        kernel_w = m.sb("kernel_w", [17, D1])
        table = [m.sb(f"table{i}", [P, NB * 2 * P]) for i in range(2)]
        spec8 = m.sb("spec8", [17, 2 * P])
        spec3 = m.sb("spec3", [17, 3, P])
        temp = m.sb("temp", [17, 2, P])
        ker = m.sb("ker", [P, 3, D1])
        v_re = m.sb("v_re", [P, B, D1])
        v_im = m.sb("v_im", [P, B, D1])
        prod = m.sb("prod", [P, 4, B, D1])
        out_f = m.sb("out_f", [P, 2 * FB, B * D1])
        spec8_ps = m.ps("spec8_ps", [16, 512])
        ker_ps = m.ps("ker_ps", [P, 2, 512])
        v_ps = m.ps("v_ps", [P, 4, 512])

        loaded = m.sem("loaded")
        table_in = [m.sem(f"table_in{i}") for i in range(2)]
        offset_in = m.sem("offset_in")
        dve_steps = m.sem("dve_steps")
        spec8_ready = m.sem("spec8_ready")
        spec3_ready = m.sem("spec3_ready")
        ker_ready = m.sem("ker_ready")
        ker_copied = m.sem("ker_copied")
        v_ready = m.sem("v_ready")
        v_copied = m.sem("v_copied")
        product_done = m.sem("product_done")
        y_ready = m.sem("y_ready")
        y_copied = m.sem("y_copied")
        block = ctx.enter_context(nc.Block())

        @block.sync
        def _(sp):
            for semaphore in (v_ready, spec3_ready, v_copied, ker_copied, product_done, ker_ready, y_ready, y_copied):
                sp.sem_inc(semaphore, 1)
            sp.dma_start(sign[:, :], a["c_sign"]).then_inc(loaded, 16)
            sp.dma_start(keep[:, :], a["c_keep"]).then_inc(loaded, 16)
            sp.dma_start(kernel_w[:, :], a["kernel_w"]).then_inc(loaded, 16)
            with sp.Fori(0, FB // 2) as f:
                for i in range(2):
                    sp.wait_ge(v_ready, f * 2 + i) if i else None
                    src = a["c_dft"][bass.ds(f * (2 * P) + i * P, P), :]
                    if not i:
                        sp.wait_ge(v_ready, f * 2 + 1)
                    sp.dma_start(table[i][:, :], src).then_inc(table_in[i], 16)
                    off = a["c_offset"][:, bass.ds(f * (4 * P) + i * 2 * P, 2 * P)]
                    sp.wait_ge(spec3_ready, f * 2 + i + 1)
                    sp.dma_start(spec8[16:17, :], off).then_inc(offset_in, 16)
            sp.wait_ge(v_ready, FB + 1)
            with sp.Fori(0, NB // 2) as t:
                for i in range(2):
                    src = a["c_idft"][bass.ds(t * (2 * P) + i * P, P), :]
                    sp.wait_ge(y_ready, t * 2 + max(i - 1, 0) + 1)
                    sp.dma_start(table[i][:, :], src).then_inc(table_in[i], 16)

        @block.tensor
        def _(pe):
            pe.wait_ge(loaded, 48)
            with pe.Fori(0, FB // 2) as f:
                for i in range(2):
                    k = f * 2 + i
                    tab = table[i][:, :].rearrange("p (t c) -> p t c", t=NB)
                    pe.wait_ge(spec3_ready, k + 1)
                    pe.wait_ge(table_in[i], f * 16 + 16)
                    for t in range(NB):
                        last = pe.matmul(spec8_ps[:, 0:2 * P], st["rpe"][:, t, :, :].rearrange("p s c -> p (s c)"),
                                         tab[:, t, :], start=(t == 0), stop=(t == NB - 1))
                    last.then_inc(spec8_ready, 1)
                    pe.wait_ge(v_copied, k + 1)
                    for half in range(2):
                        for part in range(2):
                            for t in range(NB):
                                last = pe.matmul(v_ps[:, 2 * part + half, 0:HALF], tab[:, t, part * P:(part + 1) * P],
                                                 st["v"][:, t, 2 * half:2 * half + 2, :].rearrange("p b c -> p (b c)"),
                                                 start=(t == 0), stop=(t == NB - 1))
                    last.then_inc(v_ready, 1)
                    pe.wait_ge(ker_copied, k + 1)
                    pe.wait_ge(spec3_ready, k + 2)
                    for part in range(3):
                        last = pe.matmul(ker_ps[:, part // 2, (part % 2) * D1:(part % 2 + 1) * D1], spec3[:, part, :],
                                         kernel_w[:, :], start=(part != 1), stop=(part != 0),
                                         skip_group_check=True)
                    last.then_inc(ker_ready, 1)
            pe.wait_ge(product_done, FB + 1)
            pe.wait_ge(v_copied, FB + 1)
            with pe.Fori(0, NB // 2) as t:
                for i in range(2):
                    tab = table[i][:, :].rearrange("p (f j) -> p f j", f=2 * FB)
                    pe.wait_ge(y_copied, t * 2 + max(i - 1, 0) + 1)
                    pe.wait_ge(table_in[i], t * 16 + 16 + 16 * (FB // 2))
                    for half in range(2):
                        for f in range(2 * FB):
                            last = pe.matmul(v_ps[:, 2 * i + half, 0:HALF], tab[:, f, :],
                                             out_f[:, f, half * HALF:(half + 1) * HALF],
                                             start=(f == 0), stop=(f == 2 * FB - 1))
                    last.then_inc(y_ready, 1)

        @block.scalar
        def _(act):
            with act.Fori(0, FB) as k:
                act.wait_ge(product_done, k + 1)
                act.wait_ge(v_ready, k + 2)
                act.activation(v_re[:, :, :].rearrange("p (h b) c -> p h (b c)", h=2), v_ps[:, 0:2, 0:HALF], ACT.Copy)
                act.activation(v_im[:, :, :].rearrange("p (h b) c -> p h (b c)", h=2), v_ps[:, 2:4, 0:HALF],
                               ACT.Copy).then_inc(v_copied, 1)
                act.wait_ge(ker_ready, k + 2)
                act.activation(ker[:, 0:2, :], ker_ps[:, 0, 0:2 * D1].rearrange("p (r c) -> p r c", r=2), ACT.Copy)
                act.activation(ker[:, 2, :], ker_ps[:, 1, 0:D1], ACT.Copy).then_inc(ker_copied, 1)
            with act.Fori(0, NB // 2) as t:
                for i in range(2):
                    act.wait_ge(y_ready, t * 2 + i + 2)
                    act.activation(st["y"][:, bass.ds(t * 2 + i, 1), :].rearrange("p o (h c) -> p (o h) c", h=2),
                                   v_ps[:, 2 * i:2 * i + 2, 0:HALF], ACT.Copy).then_inc(y_copied, 1)

        @block.vector
        def _(dve):
            chain = Chain(dve, dve_steps)
            dve.wait_ge(loaded, 48)
            with dve.Fori(0, FB) as k:
                dve.wait_ge(offset_in, k * 16 + 16)
                dve.wait_ge(spec8_ready, k + 1)
                chain.link(dve.tensor_tensor(spec8[0:16, :], spec8_ps[:, 0:2 * P], sign[:, bass.ds(k * (2 * P), 2 * P)],
                                             ALU.mult))
                kp = keep[:, bass.ds(k * P, P)]
                dve.wait_ge(ker_ready, k + 1)
                chain.mark(dve.tensor_copy(spec3[:, 0, :], spec8[:, 0:P]))
                chain.mark(dve.tensor_tensor(spec3[:, 1, :], spec8[:, P:2 * P], kp, ALU.mult))
                chain.link(dve.tensor_tensor(temp[:, 0, :], spec8[:, 0:P], kp, ALU.mult))
                chain.link(dve.tensor_tensor(temp[:, 1, :], spec8[:, P:2 * P], spec3[:, 1, :], ALU.subtract))
                chain.link(dve.tensor_tensor(spec3[:, 2, :], temp[:, 0, :], temp[:, 1, :], ALU.add))
                dve.sem_inc(spec3_ready, 1)
                dve.wait_ge(v_copied, k + 2)
                dve.wait_ge(ker_copied, k + 2)
                k_re, k_im, k_re2 = (bc(ker[:, i, :], 1, B) for i in range(3))
                chain.mark(dve.tensor_tensor(prod[:, 0], v_re[:, :, :], k_re, ALU.mult))
                chain.mark(dve.tensor_tensor(prod[:, 1], v_im[:, :, :], k_im, ALU.mult))
                chain.mark(dve.tensor_tensor(prod[:, 2], v_im[:, :, :], k_re2, ALU.mult))
                chain.link(dve.tensor_tensor(prod[:, 3], v_re[:, :, :], k_im, ALU.mult))
                flat = prod[:, :, :, :].rearrange("p q b c -> p q (b c)")
                chain.mark(dve.tensor_tensor(out_f[:, bass.ds(k * 2, 1), :], flat[:, 0:1], flat[:, 1:2], ALU.subtract))
                chain.link(dve.tensor_tensor(out_f[:, bass.ds(k * 2 + 1, 1), :], flat[:, 2:3], flat[:, 3:4], ALU.add))
                dve.sem_inc(product_done, 1)
                chain.clear()


def gate_stage(nc, a, st):
    with ExitStack() as ctx:
        m = Mem(nc, ctx, "gt")
        ident = m.sb("ident", [P, P])
        o_w1 = m.sb("o_w1", [P, D])
        o_w2 = m.sb("o_w2", [D1 - P + 1, D])
        t_w = m.sb("t_w", [D + 1, D])
        uy = m.sb("uy", [P, NB, D1])
        uyT1 = m.sb("uyT1", [P, N])
        uyT2 = m.sb("uyT2", [D1 - P + 1, N])
        dT = m.sb("dT", [D + 1, N])
        z = m.sb("z", [P, NB, D])
        sq = m.sb("sq", [P, NB, D])
        zn = m.sb("zn", [P, NB, D])
        xr = m.sb("xr", [P, NB, D])
        h1 = m.sb("h1", [P, NB, D])
        xc = m.sb("xc", [P, NB, D])
        xn = m.sb("xn", [P, NB, D])
        stat = m.sb("stat", [P, 4, NB])
        rms = m.sb("rms", [P, 4, NB])
        uyT1_ps = m.ps("uyT1_ps", [P, N])
        uyT2_ps = m.ps("uyT2_ps", [D1 - P, N])
        outT_ps = m.ps("outT_ps", [D, N])
        z_ps = m.ps("z_ps", [P, NB, D])

        loaded = m.sem("loaded")
        ones_set = m.sem("ones_set")
        dve_steps = m.sem("dve_steps")
        act_steps = m.sem("act_steps")
        uy_ready = m.sem("uy_ready")
        uyT_ready = m.sem("uyT_ready")
        uyT_copied = m.sem("uyT_copied")
        outT_ready = m.sem("outT_ready")
        dT_ready = m.sem("dT_ready")
        z_ready = m.sem("z_ready")
        square_ready = m.sem("square_ready")
        root_ready = m.sem("root_ready")
        zn_ready = m.sem("zn_ready")
        xr_ready = m.sem("xr_ready")
        ln_var = m.sem("ln_var")
        ln_std = m.sem("ln_std")
        xn_ready = m.sem("xn_ready")
        xnT_ready = m.sem("xnT_ready")
        xnT_copied = m.sem("xnT_copied")
        block = ctx.enter_context(nc.Block())

        @block.sync
        def _(sp):
            for semaphore in (xnT_copied, uyT_ready, xnT_ready):
                sp.sem_inc(semaphore, 1)
            sp.dma_start(ident[:, :], a["c_ident"]).then_inc(loaded, 16)
            sp.dma_start(o_w1[:, :], a["o_w"][0:P, :]).then_inc(loaded, 16)
            sp.dma_start(o_w2[:, :], a["o_w"][P:D1 + 1, :]).then_inc(loaded, 16)
            sp.dma_start(t_w[:, :], a["t_w"]).then_inc(loaded, 16)

        @block.tensor
        def _(pe):
            pe.wait_ge(loaded, 64)
            pe.wait_ge(ones_set, 2)
            with pe.Fori(0, B) as b:
                pe.wait_ge(uy_ready, b + 1)
                for t in range(NB):
                    pe.transpose(uyT1_ps[:, t * P:(t + 1) * P], uy[:, t, 0:P], ident[:, :])
                    last = pe.transpose(uyT2_ps[:, t * P:(t + 1) * P], uy[:, t, P:D1], ident[:, :])
                last.then_inc(uyT_ready, 1)
                pe.wait_ge(uyT_copied, b + 1)
                pe.wait_ge(xnT_copied, b + 1)
                for half in range(2):
                    c = slice(half * 512, half * 512 + 512)
                    pe.matmul(outT_ps[:, c], o_w1[:, :], uyT1[:, c], start=True, stop=False)
                    last = pe.matmul(outT_ps[:, c], o_w2[:, :], uyT2[:, c], start=False, stop=True)
                last.then_inc(outT_ready, 1)
                pe.wait_ge(dT_ready, b + 1)
                for t in range(NB):
                    last = pe.matmul(z_ps[:, t, :], dT[:, t * P:(t + 1) * P], t_w[:, :], start=True, stop=True)
                last.then_inc(z_ready, 1)
                pe.wait_ge(xn_ready, b + 1)
                flip_rows(pe, outT_ps, xn, ident).then_inc(xnT_ready, 1)

        @block.scalar
        def _(act):
            chain = Chain(act, act_steps)
            with act.Fori(0, B) as b:
                act.wait_ge(uyT_ready, b + 2)
                chain.mark(act.activation(uyT1[:, :], uyT1_ps[:, :], ACT.Copy))
                chain.link(act.activation(uyT2[0:D1 - P, :], uyT2_ps[:, :], ACT.Copy))
                act.sem_inc(uyT_copied, 1)
                act.wait_ge(square_ready, b + 1)
                act.activation(rms[:, 1, :], rms[:, 0, :], ACT.Sqrt).then_inc(root_ready, 1)
                act.wait_ge(zn_ready, b + 1)
                act.activation(xr[:, :, :], zn[:, :, :], ACT.Silu).then_inc(xr_ready, 1)
                act.wait_ge(ln_var, b + 1)
                act.activation(stat[:, 3, :], stat[:, 0, :], ACT.Sqrt).then_inc(ln_std, 1)
                act.wait_ge(xnT_ready, b + 2)
                act.activation(st["xnT"][:, bass.ds(b * N, N)], outT_ps[:, :], ACT.Copy).then_inc(xnT_copied, 1)
                chain.clear()

        @block.vector
        def _(dve):
            chain = Chain(dve, dve_steps)
            dve.memset(uyT2[D:D + 1, :], 1.0).then_inc(ones_set, 1)
            dve.memset(dT[D:D + 1, :], 1.0).then_inc(ones_set, 1)
            with dve.Fori(0, B) as b:
                blocks = bass.ds(b * NB, NB)
                dve.wait_ge(uyT_ready, b + 1)
                dve.tensor_tensor(uy[:, :, :], st["u"][:, blocks, :], st["y"][:, :, bass.ds(b * D1, D1)], ALU.mult)\
                   .then_inc(uy_ready, 1)
                dve.wait_ge(outT_ready, b + 1)
                dve.tensor_tensor(dT[0:D, :], st["xnT"][:, bass.ds(b * N, N)], outT_ps[:, :], ALU.subtract)\
                   .then_inc(dT_ready, 1)
                dve.wait_ge(z_ready, b + 1)
                chain.link(dve.tensor_copy(z[:, :, :], z_ps[:, :, :]))
                chain.link(dve.tensor_tensor(sq[:, :, :], z[:, :, :], z[:, :, :], ALU.mult))
                chain.link(dve.tensor_reduce(rms[:, 2, :], sq[:, :, :], AX, ALU.add))
                dve.tensor_scalar(rms[:, 0, :], rms[:, 2, :], 1.0 / D1, None, ALU.mult).then_inc(square_ready, 1)
                dve.wait_ge(root_ready, b + 1)
                chain.link(dve.tensor_scalar(rms[:, 2, :], rms[:, 1, :], RMS_EPS, None, ALU.add))
                chain.link(dve.reciprocal(rms[:, 3, :], rms[:, 2, :]))
                dve.tensor_tensor(zn[:, :, :], z[:, :, :], bc(rms[:, 3, :], 2, D), ALU.mult).then_inc(zn_ready, 1)
                chain.link(dve.tensor_tensor(h1[:, :, :], st["h"][:, blocks, :], st["xn"][:, blocks, :], ALU.add))
                dve.wait_ge(xr_ready, b + 1)
                chain.link(dve.tensor_tensor(xc[:, :, :], h1[:, :, :], xr[:, :, :], ALU.add))
                chain.link(dve.tensor_copy(st["h"][:, blocks, :], xc[:, :, :]))
                layernorm_a(dve, chain, xc[:, :, :], h1[:, :, :], sq[:, :, :], stat)
                dve.tensor_copy(stat[:, 0, :], stat[:, 2, :]).then_inc(ln_var, 1)
                dve.wait_ge(ln_std, b + 1)
                chain.link(dve.reciprocal(stat[:, 1, :], stat[:, 3, :]))
                dve.wait_ge(xnT_ready, b + 1)
                chain.link(dve.tensor_tensor(xn[:, :, :], h1[:, :, :], bc(stat[:, 1, :], 2, D), ALU.mult))
                dve.sem_inc(xn_ready, 1)
                chain.link(dve.tensor_copy(st["xn"][:, blocks, :], xn[:, :, :]))
                chain.clear()


RING = 4
HALF_N = N // 2
KV_BLOCKS = [[(i, c) for i in range(NB) for c in range(2) if i >= 4 * c],
             [(i, c) for i in range(NB) for c in range(2)]]
FIRST_PASS = {True: KV_BLOCKS[0], False: KV_BLOCKS[1]}
SECOND_PASS = {True: [(0, j) for j in range(4)] + [(1, j) for j in range(NB)],
               False: [(c, j) for c in range(2) for j in range(NB)]}


def attention_units(causal):
    return 4 + len(FIRST_PASS[causal]) + 2 + len(SECOND_PASS[causal]) + 2


A_UNITS = attention_units(True)
L1_UNITS = attention_units(False)
FINISH_UNITS = 2 + L1_UNITS + 2 + 8 + NB
assert A_UNITS % RING == 0 and FINISH_UNITS % RING == 0 and (2 + L1_UNITS) % 2 == 0
A_TURNS, F_TURNS = A_UNITS // RING, FINISH_UNITS // RING
BATCH_TURNS = H * A_TURNS + F_TURNS


def cols_first(i, c, causal):
    return c * HALF_N, min((i + 1) * P, (c + 1) * HALF_N) if causal else (c + 1) * HALF_N


def cols_second(c, j, causal):
    return (max(c * HALF_N, j * P) if causal else c * HALF_N), (c + 1) * HALF_N


class Ring:

    def __init__(self, turns):
        self.turns = turns

    def bank(self, u):
        return u % RING

    def ready(self, u):
        return self.turns * RING + (u + 2)

    def free_before(self, u):
        return self.turns + (u // RING + 1)

    def free_after(self, u):
        return self.turns + (u // RING + 2)


def mixer_stage(nc, a, st, out):
    with ExitStack() as ctx:
        m = Mem(nc, ctx, "mx")
        kv_d = nc.dram_tensor("kv_scratch", (TB * H * P, 2 * D), F32).ap()
        kv_by_head = kv_d.rearrange("(s x) c -> x s c", x=H * P)
        ident = m.sb("ident", [P, P])
        ident_b = m.sb("ident_b", [P, P], BF16)
        causal = m.sb("causal", [P, 2, P])
        causal_b = m.sb("causal_b", [P, 2, P], BF16)
        pk_w = m.sb("pk_w", [D, 4 * P])
        keys = m.sb("keys", [P, 4, 4 * NK])
        rank = m.sb("rank", [P, CAND])
        head_base = m.sb("head_base", [P, H, TOPK])
        expert_id = m.sb("expert_id", [P, E])
        l1_w = m.sb("l1_w", [D, 2, P])
        router = m.sb("router", [D, E])
        w1 = m.sb("w1", [D + 1, E * D])
        w2 = m.sb("w2", [P, E // 2, P])
        b2 = m.sb("b2", [1, E * D])
        ones = m.sb("ones", [1, P])
        xb = m.sb("xb", [D, P])
        qT_pk = m.sb("qT_pk", [P, 4, P])
        S = m.sb("S", [P, 2 * H, NK])
        S2 = m.sb("S2", [P, 2 * H, NK])
        V = m.sb("V", [P, 2 * H, TOPK])
        I = m.sb("I", [P, 2 * H, TOPK], U32)
        If = m.sb("If", [P, 2 * H, TOPK])
        C = m.sb("C", [P, H, CAND])
        C2 = m.sb("C2", [P, H, CAND])
        CI = m.sb("CI", [P, H, CAND])
        FV = m.sb("FV", [P, H, TOPK])
        FI = m.sb("FI", [P, H, TOPK], U32)
        FIf = m.sb("FIf", [P, H, TOPK])
        hot = m.sb("hot", [P, 2, TOPK, CAND])
        e_in = m.sb("e_in", [P, H, TOPK])
        e_out = m.sb("e_out", [P, H, TOPK])
        e_sum = m.sb("e_sum", [P, 2, H])
        next_w = m.sb("next_w", [P, H, TOPK])
        next_i = m.sb("next_i", [P, H, TOPK], U32)
        slot_w = m.sb("slot_w", [P, H, TOPK])
        slot_i = m.sb("slot_i", [P, H, TOPK], U32)
        G = m.sb("G", [P, H, TOPK, 2 * D])
        kv = m.sb("kv", [P, H, 2 * D])
        kvt = m.sb("kvt", [P, NB, 2 * D + 1])
        q_w = m.sb("q_w", [D, P])
        o_w = m.sb("o_w", [D + 1, D + 1])
        xT = m.sb("xT", [D, N])
        kT = m.sb("kT", [D + 1, N])
        qT = m.sb("qT", [D + 1, N])
        part_max = m.sb("part_max", [P, 2, NB, 2])
        row_max = m.sb("row_max", [P, NB])
        minus_max = m.sb("minus_max", [P, NB, D + 1])
        pT = m.sb("pT", [P, 2, HALF_N])
        oT = m.sb("oT", [D + 1, N])
        rz = m.sb("rz", [P, NB // 2])
        o_tmp = m.sb("o_tmp", [P, NB // 2, D])
        acc = m.sb("acc", [P, NB, D])
        xc = m.sb("xc", [P, NB, D])
        sq = m.sb("sq", [P, NB, D])
        stat = m.sb("stat", [P, 4, NB])
        x3 = m.sb("x3", [P, NB, D + 1])
        x3T = m.sb("x3T", [D, N])
        x4 = m.sb("x4", [P, NB, D])
        x4T = m.sb("x4T", [D + 1, N])
        lg = m.sb("lg", [P, NB, E])
        pr = m.sb("pr", [P, NB, E])
        pv = m.sb("pv", [P, NB, E])
        pi = m.sb("pi", [P, NB, E], U32)
        pif = m.sb("pif", [P, NB, E])
        comb = m.sb("comb", [P, 2, NB, E])
        gate = m.sb("gate", [P, NB, E])
        r8 = m.sb("r8", [P, 2, NB])
        hT = m.sb("hT", [P, E // 2, N])
        yw = m.sb("yw", [P, E, D])
        out_sb = m.sb("out_sb", [P, NB, D])
        q_ps = m.ps("q_ps", [P, 4, P])
        sim_ps = m.ps("sim_ps", [P, 2 * H, NK])
        ring = m.ps("ring", [P, RING, 512])
        o_ps = m.ps("o_ps", [P, 512])

        loaded = m.sem("loaded")
        consts_set = m.sem("consts_set")
        dve_steps = m.sem("dve_steps")
        act_steps = m.sem("act_steps")
        xb_ready = m.sem("xb_ready")
        q_ready = m.sem("q_ready")
        q_copied = m.sem("q_copied")
        sim_ready = m.sem("sim_ready")
        sim_taken = m.sem("sim_taken")
        e_in_ready = m.sem("e_in_ready")
        e_out_ready = m.sem("e_out_ready")
        slot_ready = m.sem("slot_ready")
        slot_seen = m.sem("slot_seen")
        gathered = [m.sem(f"gathered{h}") for h in range(H)]
        kv_ready = m.sem("kv_ready")
        kv_stored = m.sem("kv_stored")
        a_in = m.sem("a_in")
        unit_ready = m.sem("unit_ready")
        bank_free = [m.sem(f"bank_free{i}") for i in range(RING)]
        max_ready = m.sem("max_ready")
        o_ready = m.sem("o_ready")
        o_taken = m.sem("o_taken")
        ln_var = m.sem("ln_var")
        ln_std = m.sem("ln_std")
        rows_ready = m.sem("rows_ready")
        logits_ready = m.sem("logits_ready")
        route_in = m.sem("route_in")
        route_out = m.sem("route_out")
        out_ready = m.sem("out_ready")
        out_stored = m.sem("out_stored")
        block = ctx.enter_context(nc.Block())
        N_LOADS = 13

        @block.sync
        def _(sp):
            for semaphore in (*bank_free, q_ready, sim_ready, sim_taken, kv_stored, unit_ready, o_taken, out_stored):
                sp.sem_inc(semaphore, 1)
            for dst, src in (
                (ident[:, :], a["c_ident"]), (causal[:, 0, :], a["c_causal"]), (causal[:, 1, :], a["c_causalT"]),
                (pk_w[:, :], a["pk_w"]), (keys[:, :, :], a["pk_keys"].rearrange("p (c k) -> p c k", c=4)),
                (rank[:, :], a["c_rank"]), (head_base[:, :, :], a["c_head"].rearrange("p (h r) -> p h r", h=H)),
                (expert_id[:, :], a["c_expert"]), (l1_w[:, :, :], a["l1_w"].rearrange("p (c k) -> p c k", c=2)),
                (router[:, :], a["router_w"]), (w1[:, :], a["w1"]),
                (w2[:, :, :], a["w2"].rearrange("p (c k) -> p c k", c=E // 2)), (b2[:, :], a["b2"]),
            ):
                sp.dma_start(dst, src).then_inc(loaded, 16)

            def store_kv(g):
                dst = kv_d[bass.ds(g * (H * P), H * P), :].rearrange("(h p) c -> p h c", p=P)
                sp.wait_ge(kv_ready, g + 1)
                sp.dma_start(dst, kv[:, :, :]).then_inc(kv_stored, 16)

            def load_head(b, h):
                src = kv_by_head[bass.ds(h * P, P), bass.ds(b * NB, NB), :]
                sp.wait_ge(unit_ready, (b * BATCH_TURNS + h * A_TURNS) * RING + 1)
                sp.wait_ge(kv_stored, (b + 1) * (16 * NB) + 1)
                sp.dma_start(kvt[:, :, 0:2 * D], src).then_inc(a_in, 16)
                sp.dma_start(q_w[:, 0:D], a["q_w"][bass.ds(h * D, D), :]).then_inc(a_in, 16)
                sp.dma_start(o_w[:, :], a["out_proj"][bass.ds(h * (D + 1), D + 1), :]).then_inc(a_in, 16)
                sp.dma_start(xT[:, :], st["xnT"][:, bass.ds(b * N, N)]).then_inc(a_in, 16)

            def store_out(b):
                dst = out[bass.ds(b * N, N), :].rearrange("(t p) d -> p t d", p=P)
                sp.wait_ge(out_ready, b + 1)
                sp.dma_start(dst, out_sb[:, :, :]).then_inc(out_stored, 16)

            with sp.Fori(1, NB) as g:
                store_kv(g - 1)
            with sp.Fori(0, B - 1) as b:
                with sp.Fori(0, H) as h:
                    store_kv(b * NB + h + (NB - 1))
                    load_head(b, h)
                store_out(b)
            store_kv(TB - 1)
            with sp.Fori(0, H) as h:
                load_head(B - 1, h)
            store_out(B - 1)
            sp.wait_ge(out_stored, 16 * B + 1)
            sp.wait_ge(kv_stored, 16 * TB + 1)

        @block.gpsimd
        def _(pool):
            with pool.Fori(0, TB) as g:
                for h in range(H):
                    pool.wait_ge(slot_ready, g * H + h + 1)
                    pool.sem_inc(slot_seen, 1)
                    for r in range(TOPK):
                        pool.indirect_dma_start(G[:, h, r, :], None, a["kv_table"],
                                                bass.IndirectOffsetOnAxis(slot_i[:, h, r:r + 1], 0))\
                            .then_inc(gathered[h], 16)

        @block.tensor
        def _(pe):
            pe.wait_ge(loaded, 16 * N_LOADS)
            pe.wait_ge(consts_set, 1)

            def T(g):
                pe.wait_ge(xb_ready, g + 1)
                for c in range(4):
                    last = pe.matmul(q_ps[:, c, :], pk_w[:, c * P:(c + 1) * P], xb[:, :], start=True, stop=True)
                last.then_inc(q_ready, 1)
                pe.wait_ge(q_copied, g + 1)
                pe.wait_ge(sim_taken, g + 1)
                for c in range(4):
                    last = pe.matmul(sim_ps[:, 4 * c:4 * c + 4, :].rearrange("p a k -> p (a k)"), qT_pk[:, c, :],
                                     keys[:, c, :], start=True, stop=True)
                last.then_inc(sim_ready, 1)

            def attend(rg, u, is_causal, k_part, value, o_weights, o_count, max_count):
                def begin(u):
                    pe.wait_ge(bank_free[rg.bank(u)], rg.free_before(u))
                    return ring[:, rg.bank(u), :]

                for half in range(2):
                    k_part(half, begin(u)).then_inc(unit_ready, 1)
                    u += 1
                weights, source = (q_w[:, :], xT) if is_causal else (l1_w[:, 0, :], x3T)
                for half in range(2):
                    pe.matmul(begin(u), weights, source[:, half * HALF_N:(half + 1) * HALF_N],
                              start=True, stop=True).then_inc(unit_ready, 1)
                    u += 1
                for v in range(u - 4, u):
                    pe.wait_ge(bank_free[rg.bank(v)], rg.free_after(v))
                for i, c in FIRST_PASS[is_causal]:
                    lo, hi = cols_first(i, c, is_causal)
                    bank = begin(u)
                    diagonal = is_causal and hi == (i + 1) * P
                    last = pe.matmul(bank[:, 0:hi - lo], qT[0:D, i * P:(i + 1) * P], kT[0:D, lo:hi],
                                     start=True, stop=not diagonal, skip_group_check=True)
                    if diagonal:
                        last = pe.matmul(bank[:, hi - lo - P:hi - lo], ident_b[:, :], causal_b[:, 0, :],
                                         start=False, stop=True, skip_group_check=True)
                    last.then_inc(unit_ready, 1)
                    u += 1
                pe.wait_ge(max_ready, max_count)
                for half in range(2):
                    bank = begin(u)
                    for t in range(4):
                        last = pe.matmul(bank[0:D + 1, t * P:(t + 1) * P], minus_max[:, 4 * half + t, :], ident[:, :],
                                         start=True, stop=True)
                    last.then_inc(unit_ready, 1)
                    u += 1
                for v in range(u - 2, u):
                    pe.wait_ge(bank_free[rg.bank(v)], rg.free_after(v))

                def weigh(v, c, j):
                    lo, hi = cols_second(c, j, is_causal)
                    first, final = j == 0, j == (3 if is_causal and c == 0 else NB - 1)
                    if first:
                        pe.wait_ge(o_taken, o_count + c + 1)
                    pe.wait_ge(bank_free[rg.bank(v)], rg.free_after(v))
                    last = pe.matmul(o_ps[0:D + 1, lo - c * HALF_N:hi - c * HALF_N], value[:, j, :],
                                     pT[:, v % 2, 0:hi - lo], start=first, stop=final, skip_group_check=True)
                    if final:
                        last.then_inc(o_ready, 1)

                before = None
                for c, j in SECOND_PASS[is_causal]:
                    lo, hi = cols_second(c, j, is_causal)
                    bank = begin(u)
                    diagonal = is_causal and lo == j * P
                    last = pe.matmul(bank[:, 0:hi - lo], kT[:, j * P:(j + 1) * P], qT[:, lo:hi],
                                     start=True, stop=not diagonal, skip_group_check=True)
                    if diagonal:
                        last = pe.matmul(bank[:, 0:P], ident_b[:, :], causal_b[:, 1, :],
                                         start=False, stop=True, skip_group_check=True)
                    last.then_inc(unit_ready, 1)
                    if before:
                        weigh(*before)
                    before = (u, c, j)
                    u += 1
                weigh(*before)
                for half in range(2):
                    pe.wait_ge(o_taken, o_count + (half + 1) + 1)
                    bank = begin(u)
                    for t in range(4):
                        at = half * HALF_N + t * P
                        last = pe.matmul(bank[:, t * (D + 1):(t + 1) * (D + 1)], oT[:, at:at + P], o_weights,
                                         start=True, stop=True)
                    last.then_inc(unit_ready, 1)
                    u += 1
                return u

            def A(b, h):
                rg = Ring(b * BATCH_TURNS + h * A_TURNS)
                q = b * H + h
                pe.wait_ge(a_in, q * 64 + 64)

                def k_part(half, bank):
                    for t in range(4):
                        last = pe.matmul(bank[0:D, t * P:(t + 1) * P], kvt[:, 4 * half + t, 0:D], ident[:, :],
                                         start=True, stop=True)
                    return last

                attend(rg, 0, True, k_part, kvt[:, :, D:2 * D + 1], o_w[:, :], b * (2 * H + 2) + h * 2,
                       b * (H + 1) + h + 1)

            def F(b):
                rg = Ring(b * BATCH_TURNS + H * A_TURNS)
                u = 0

                def begin(u):
                    pe.wait_ge(bank_free[rg.bank(u)], rg.free_before(u))
                    return ring[:, rg.bank(u), :]

                def flip(x, u):
                    for half in range(2):
                        bank = begin(u)
                        for t in range(4):
                            last = pe.matmul(bank[0:D, t * P:(t + 1) * P], x[:, 4 * half + t, 0:D], ident[:, :],
                                             start=True, stop=True)
                        last.then_inc(unit_ready, 1)
                        u += 1
                    for v in range(u - 2, u):
                        pe.wait_ge(bank_free[rg.bank(v)], rg.free_after(v))
                    return u

                pe.wait_ge(rows_ready, b * 2 + 1)
                u = flip(x3, u)

                def k_part(half, bank):
                    return pe.matmul(bank, l1_w[:, 1, :], x3T[:, half * HALF_N:(half + 1) * HALF_N],
                                     start=True, stop=True)

                u = attend(rg, u, False, k_part, x3[:, :, :], ident[0:D + 1, 0:D + 1], b * (2 * H + 2) + 2 * H,
                           b * (H + 1) + H + 1)
                pe.wait_ge(rows_ready, b * 2 + 2)
                u = flip(x4, u)
                for t in range(NB):
                    last = pe.matmul(o_ps[:, t * E:(t + 1) * E], x4T[0:D, t * P:(t + 1) * P], router[:, :],
                                     start=True, stop=True)
                last.then_inc(logits_ready, 1)
                for e2 in range(E // 2):
                    for half in range(2):
                        pe.matmul(begin(u), w1[:, e2 * P:(e2 + 1) * P], x4T[:, half * HALF_N:(half + 1) * HALF_N],
                                  start=True, stop=True).then_inc(unit_ready, 1)
                        u += 1
                for v in range(u - 4, u):
                    pe.wait_ge(bank_free[rg.bank(v)], rg.free_after(v))
                for t in range(NB):
                    bank = begin(u)
                    pe.matmul(bank, ones[:, :], b2[:, :], start=True, stop=False, skip_group_check=True)
                    for e2 in range(E // 2):
                        last = pe.matmul(bank[:, e2 * P:(e2 + 1) * P], hT[:, e2, t * P:(t + 1) * P], w2[:, e2, :],
                                         start=False, stop=True, skip_group_check=True)
                    last.then_inc(unit_ready, 1)
                    u += 1
                assert u == FINISH_UNITS

            with pe.Fori(0, NB) as g:
                T(g)
            with pe.Fori(0, B - 1) as b:
                with pe.Fori(0, H) as h:
                    T(b * NB + h + NB)
                    A(b, h)
                F(b)
            with pe.Fori(0, H) as h:
                A(B - 1, h)
            F(B - 1)

        @block.scalar
        def _(act):
            def T(g):
                act.wait_ge(q_ready, g + 1)
                act.activation(xb[:, :], st["xnT"][:, bass.ds(g * P, P)], ACT.Copy).then_inc(xb_ready, 1)
                act.wait_ge(q_ready, g + 2)
                act.wait_ge(sim_ready, g + 1)
                act.activation(qT_pk[:, :, :], q_ps[:, :, :], ACT.Copy).then_inc(q_copied, 1)
                act.wait_ge(e_in_ready, g + 1)
                act.activation(e_out[:, :, :], e_in[:, :, :], ACT.Exp).then_inc(e_out_ready, 1)

            def take(rg, u, out_ap, in_rows, n, func=ACT.Copy, scale=1.0):
                act.wait_ge(unit_ready, rg.ready(u))
                act.activation(out_ap, ring[in_rows, rg.bank(u), 0:n], func, scale=scale)\
                   .then_inc(bank_free[rg.bank(u)], 1)

            def attend(rg, u, is_causal, o_count):
                for half in range(2):
                    take(rg, u + half, kT[0:D, half * HALF_N:(half + 1) * HALF_N], slice(0, D), HALF_N)
                for half in range(2):
                    take(rg, u + 2 + half, qT[0:D, half * HALF_N:(half + 1) * HALF_N], slice(0, D), HALF_N,
                         scale=float(D) ** -0.5)
                u += 4 + len(FIRST_PASS[is_causal])
                for half in range(2):
                    take(rg, u, qT[D:D + 1, half * HALF_N:(half + 1) * HALF_N], slice(D, D + 1), HALF_N)
                    u += 1

                def take_o(c):
                    act.wait_ge(o_ready, o_count + c + 1)
                    act.activation(oT[:, c * HALF_N:(c + 1) * HALF_N], o_ps[0:D + 1, :], ACT.Copy)\
                       .then_inc(o_taken, 1)

                for c, j in SECOND_PASS[is_causal]:
                    lo, hi = cols_second(c, j, is_causal)
                    if c == 1 and j == 1:
                        take_o(0)
                    take(rg, u, pT[:, u % 2, 0:hi - lo], slice(0, P), hi - lo, func=ACT.Exp)
                    u += 1
                take_o(1)
                return u + 2

            def A(b, h):
                attend(Ring(b * BATCH_TURNS + h * A_TURNS), 0, True, b * (2 * H + 2) + h * 2)

            def F(b):
                rg = Ring(b * BATCH_TURNS + H * A_TURNS)
                u = 0
                for n, dst in enumerate((x3T, x4T)):
                    act.wait_ge(ln_var, b * 2 + n + 1)
                    act.activation(stat[:, 3, :], stat[:, 0, :], ACT.Sqrt).then_inc(ln_std, 1)
                    for half in range(2):
                        take(rg, u, dst[0:D, half * HALF_N:(half + 1) * HALF_N], slice(0, D), HALF_N)
                        u += 1
                    if n == 0:
                        u = attend(rg, u, False, b * (2 * H + 2) + 2 * H)
                act.wait_ge(route_in, b + 1)
                act.activation(pr[:, :, :], lg[:, :, :], ACT.Exp).then_inc(route_out, 1)
                for e2 in range(E // 2):
                    for half in range(2):
                        take(rg, u, hT[:, e2, half * HALF_N:(half + 1) * HALF_N], slice(0, P), HALF_N, func=ACT.Gelu)
                        u += 1

            with act.Fori(0, NB) as g:
                T(g)
            with act.Fori(0, B - 1) as b:
                with act.Fori(0, H) as h:
                    T(b * NB + h + NB)
                    A(b, h)
                F(b)
            with act.Fori(0, H) as h:
                A(B - 1, h)
            F(B - 1)

        @block.vector
        def _(dve):
            chain = Chain(dve, dve_steps)
            dve.wait_ge(loaded, 16 * N_LOADS)
            chain.mark(dve.tensor_copy(ident_b[:, :], ident[:, :]))
            chain.mark(dve.tensor_copy(causal_b[:, :, :], causal[:, :, :]))
            chain.mark(dve.memset(kvt[:, :, 2 * D:2 * D + 1], 1.0))
            chain.mark(dve.memset(q_w[:, D:P], 0.0))
            chain.mark(dve.memset(kT[D:D + 1, :], 1.0))
            chain.mark(dve.memset(part_max[:, :, :, :], LOWEST))
            chain.mark(dve.memset(minus_max[:, :, :], 0.0))
            chain.mark(dve.memset(x3[:, :, D:D + 1], 1.0))
            chain.mark(dve.memset(x4T[D:D + 1, :], 1.0))
            chain.link(dve.memset(ones[:, :], 1.0))
            dve.sem_inc(consts_set, 1)
            chain.clear()

            def best(values, again, found, where, n):
                for j in range(n):
                    chain.mark(dve.max(found[:, j, 0:8], values[:, j, :]))
                chain.wait()
                for j in range(n):
                    chain.mark(dve.max_index(where[:, j, 0:8], found[:, j, 0:8], values[:, j, :]))
                    chain.mark(dve.match_replace(again[:, j, :], found[:, j, 0:8], values[:, j, :], LOWEST))
                chain.wait()
                for j in range(n):
                    chain.mark(dve.max(found[:, j, 8:16], again[:, j, :]))
                chain.wait()
                for j in range(n):
                    chain.mark(dve.max_index(where[:, j, 8:16], found[:, j, 8:16], again[:, j, :]))
                chain.wait()

            def T(g):
                dve.wait_ge(sim_ready, g + 2)
                chain.link(dve.tensor_copy(S[:, :, :], sim_ps[:, :, :]))
                dve.sem_inc(sim_taken, 1)
                best(S, S2, V, I, 2 * H)
                chain.link(dve.tensor_copy(If[:, :, :], I[:, :, :]))
                chain.link(dve.tensor_scalar(If[:, H:2 * H, :], If[:, H:2 * H, :], float(NK), None, ALU.mult))
                chain.link(dve.tensor_tensor(If[:, H:2 * H, :], If[:, H:2 * H, :], head_base[:, :, :], ALU.add))
                at = 0
                for a0, na, nb in RECTS:
                    for dst, src in ((C, V), (CI, If)):
                        chain.mark(dve.tensor_tensor(
                            dst[:, :, at:at + na * nb].rearrange("p h (x y) -> p h x y", y=nb),
                            bc(src[:, 0:H, a0:a0 + na], 3, nb), bc(src[:, H:2 * H, 0:nb], 2, na), ALU.add))
                    at += na * nb
                chain.wait()
                best(C, C2, FV, FI, H)
                chain.mark(dve.tensor_tensor(e_in[:, :, :], FV[:, :, :], FV[:, :, 0:1].broadcast_to([P, H, TOPK]),
                                             ALU.subtract))
                chain.link(dve.tensor_copy(FIf[:, :, :], FI[:, :, :]))
                dve.sem_inc(e_in_ready, 1)
                for part in range(H // 2):
                    hs = slice(part * 2, part * 2 + 2)
                    chain.link(dve.tensor_tensor(hot[:, :, :, :], bc(FIf[:, hs, :], 3, CAND),
                                                 bc(bc(rank[:, :], 1, TOPK), 1, 2), ALU.is_equal))
                    chain.link(dve.tensor_tensor(hot[:, :, :, :], hot[:, :, :, :], bc(CI[:, hs, :], 2, TOPK), ALU.mult))
                    chain.link(dve.tensor_reduce(FIf[:, hs, :], hot[:, :, :, :], AX, ALU.add))
                chain.mark(dve.tensor_copy(next_i[:, :, :], FIf[:, :, :]))
                dve.wait_ge(e_out_ready, g + 1)
                chain.link(dve.tensor_reduce(e_sum[:, 0, :], e_out[:, :, :], AX, ALU.add))
                chain.link(dve.reciprocal(e_sum[:, 1, :], e_sum[:, 0, :]))
                chain.link(dve.tensor_tensor(next_w[:, :, :], e_out[:, :, :], bc(e_sum[:, 1, :], 2, TOPK), ALU.mult))

            def install(h):
                chain.mark(dve.tensor_copy(slot_w[:, h, :], next_w[:, h, :]))
                chain.link(dve.tensor_copy(slot_i[:, h, :], next_i[:, h, :]))
                dve.sem_inc(slot_ready, 1)

            def combine(g, more):
                dve.wait_ge(kv_stored, g * 16 + 1)
                for h in range(H):
                    dve.wait_ge(gathered[h], g * (16 * TOPK) + 16 * TOPK)
                    chain.link(dve.tensor_tensor(G[:, h, :, :], G[:, h, :, :], bc(slot_w[:, h, :], 2, 2 * D), ALU.mult))
                    chain.link(dve.tensor_reduce(kv[:, h, :], G[:, h, :, :].rearrange("p r d -> p d r"), AX, ALU.add))
                    if more:
                        install(h)
                dve.sem_inc(kv_ready, 1)

            def attend(rg, u, is_causal, which, max_count):
                u += 4
                for i, c in FIRST_PASS[is_causal]:
                    lo, hi = cols_first(i, c, is_causal)
                    dve.wait_ge(unit_ready, rg.ready(u))
                    dve.tensor_reduce(part_max[:, which, i, c:c + 1], ring[:, rg.bank(u), 0:hi - lo], AX, ALU.max)\
                       .then_inc(bank_free[rg.bank(u)], 1)
                    u += 1
                for v in range(u - 4, u):
                    dve.wait_ge(bank_free[rg.bank(v)], rg.free_after(v))
                chain.link(dve.tensor_reduce(row_max[:, :], part_max[:, which, :, :], AX, ALU.max))
                dve.tensor_scalar(minus_max[:, :, D], row_max[:, :], -1.0, None, ALU.mult).then_inc(max_ready, 1)
                u += 2 + len(SECOND_PASS[is_causal])
                for half in range(2):
                    bank = ring[:, rg.bank(u), 0:4 * (D + 1)].rearrange("p (t c) -> p t c", c=D + 1)
                    dve.wait_ge(unit_ready, rg.ready(u))
                    chain.link(dve.reciprocal(rz[:, :], bank[:, :, D]))
                    chain.link(dve.tensor_tensor(o_tmp[:, :, :], bank[:, :, 0:D], bc(rz[:, :], 2, D), ALU.mult))
                    dve.sem_inc(bank_free[rg.bank(u)], 1)
                    part = acc[:, 4 * half:4 * half + 4, :]
                    chain.link(dve.tensor_tensor(part, part, o_tmp[:, :, :], ALU.add))
                    u += 1
                return u

            def start_batch(b):
                chain.link(dve.tensor_copy(acc[:, :, :], st["h"][:, bass.ds(b * NB, NB), :]))

            def A(b, h):
                attend(Ring(b * BATCH_TURNS + h * A_TURNS), 0, True, 0, None)

            def norm(b, n, dst):
                layernorm_a(dve, chain, acc[:, :, :], xc[:, :, :], sq[:, :, :], stat)
                dve.tensor_copy(stat[:, 0, :], stat[:, 2, :]).then_inc(ln_var, 1)
                dve.wait_ge(ln_std, b * 2 + n + 1)
                chain.link(dve.reciprocal(stat[:, 1, :], stat[:, 3, :]))
                chain.link(dve.tensor_tensor(dst, xc[:, :, :], bc(stat[:, 1, :], 2, D), ALU.mult))
                dve.sem_inc(rows_ready, 1)

            def F(b):
                rg = Ring(b * BATCH_TURNS + H * A_TURNS)
                norm(b, 0, x3[:, :, 0:D])
                u = attend(rg, 2, False, 1, None)
                norm(b, 1, x4[:, :, :])
                u += 2
                dve.wait_ge(logits_ready, b + 1)
                chain.link(dve.tensor_copy(gate[:, :, :], o_ps[:, 0:NB * E].rearrange("p (t e) -> p t e", e=E)))
                chain.link(dve.tensor_reduce(r8[:, 0, :], gate[:, :, :], AX, ALU.max))
                dve.tensor_tensor(lg[:, :, :], gate[:, :, :], bc(r8[:, 0, :], 2, E), ALU.subtract)\
                   .then_inc(route_in, 1)
                dve.wait_ge(route_out, b + 1)
                chain.link(dve.tensor_reduce(r8[:, 1, :], pr[:, :, :], AX, ALU.add))
                chain.link(dve.reciprocal(r8[:, 0, :], r8[:, 1, :]))
                chain.link(dve.tensor_tensor(gate[:, :, :], pr[:, :, :], bc(r8[:, 0, :], 2, E), ALU.mult))
                for t in range(NB):
                    chain.mark(dve.max(pv[:, t, :], gate[:, t, :]))
                chain.wait()
                for t in range(NB):
                    chain.mark(dve.max_index(pi[:, t, :], pv[:, t, :], gate[:, t, :]))
                chain.wait()
                chain.mark(dve.tensor_copy(pif[:, :, :], pi[:, :, :]))
                chain.link(dve.tensor_tensor(r8[:, 0, :], pv[:, :, 0], pv[:, :, 1], ALU.add))
                chain.link(dve.tensor_scalar(r8[:, 0, :], r8[:, 0, :], 1e-12, None, ALU.max))
                chain.link(dve.reciprocal(r8[:, 1, :], r8[:, 0, :]))
                for k in range(2):
                    chain.link(dve.tensor_tensor(comb[:, k], bc(expert_id[:, :], 1, NB),
                                                 pif[:, :, k:k + 1].broadcast_to([P, NB, E]), ALU.is_equal))
                    chain.link(dve.tensor_tensor(comb[:, k], comb[:, k], pv[:, :, k:k + 1].broadcast_to([P, NB, E]),
                                                 ALU.mult))
                chain.link(dve.tensor_tensor(comb[:, 0], comb[:, 0], comb[:, 1], ALU.add))
                chain.link(dve.tensor_tensor(gate[:, :, :], comb[:, 0], bc(r8[:, 1, :], 2, E), ALU.mult))
                u += 8
                for t in range(NB):
                    dve.wait_ge(unit_ready, rg.ready(u))
                    chain.link(dve.tensor_tensor(yw[:, :, :], ring[:, rg.bank(u), :].rearrange("p (e d) -> p e d", e=E),
                                                 bc(gate[:, t, :], 2, D), ALU.mult))
                    dve.sem_inc(bank_free[rg.bank(u)], 1)
                    chain.link(dve.tensor_reduce(sq[:, t, :], yw[:, :, :].rearrange("p e d -> p d e"), AX, ALU.add))
                    u += 1
                chain.link(dve.tensor_tensor(sq[:, :, :], sq[:, :, :], x4[:, :, :], ALU.add))
                dve.wait_ge(out_stored, b * 16 + 1)
                chain.link(dve.tensor_tensor(out_sb[:, :, :], sq[:, :, :], acc[:, :, :], ALU.add))
                dve.sem_inc(out_ready, 1)

            T(0)
            for h in range(H):
                install(h)
            chain.clear()
            with dve.Fori(1, NB) as g:
                T(g)
                combine(g - 1, True)
                chain.clear()
            with dve.Fori(0, B - 1) as b:
                start_batch(b)
                chain.clear()
                with dve.Fori(0, H) as h:
                    g = b * NB + h + NB
                    T(g)
                    combine(g - 1, True)
                    A(b, h)
                    chain.clear()
                F(b)
                chain.clear()
            combine(TB - 1, False)
            start_batch(B - 1)
            chain.clear()
            with dve.Fori(0, H) as h:
                A(B - 1, h)
                chain.clear()
            F(B - 1)


def tower(nc, a, out, stages=99, probe=None):
    with ExitStack() as ctx:
        m = Mem(nc, ctx, "st")
        st = {
            "h": m.sb("h", [P, TB, D]),
            "xnT": m.sb("xnT", [D, T]),
        }
        with ExitStack() as toeplitz:
            mt = Mem(nc, toeplitz, "tz")
            st["u"] = mt.sb("u", [P, TB, D1])
            st["xn"] = mt.sb("xn", [P, TB, D])
            st["v"] = mt.sb("v", [P, NB, B, D1])
            st["y"] = mt.sb("y", [P, NB, B * D1])
            st["rpe"] = mt.sb("rpe", [P, NB, 2, RPE])
            embed_stage(nc, a, st)
            if stages == 1: return probe(nc, m, st)
            conv_stage(nc, a, st)
            if stages == 2: return probe(nc, m, st)
            gate_stage(nc, a, st)
            if stages == 3: return probe(nc, m, st)
        mixer_stage(nc, a, st, out)


def data_layout(inputs):
    f = {k: np.ascontiguousarray(v) for k, v in inputs.items()}
    row = lambda *v: np.concatenate([f[n].reshape(-1) for n in v])[None, :]
    A = "L0_attn_"
    keys = np.zeros((4, DK, 4, 4, NK), np.float32)
    for c in range(4):
        for i in range(4):
            keys[i, :, c, i, :] = f["L0_ffn_pk_keys"][c // 2, :, 4 * (c % 2) + i, :].T
    out_proj = np.zeros((H, D + 1, D + 1), np.float32)
    out_proj[:, :D, :D] = f["L0_ffn_Wo"].reshape(H, D, D)
    out_proj[:, D, D] = 1.0
    l1_w = np.zeros((D, 2, P), np.float32)
    l1_w[:, 0, :D], l1_w[:, 1, :D] = f["L1_attn_Wq"].T, f["L1_attn_Wk"].T
    w2 = np.zeros((2, D, E // 2, 2, D), np.float32)
    for e in range(E):
        w2[e % 2, :, e // 2, e % 2, :] = f["L1_ffn_w2"][e]
    d = {
        "ids": np.ascontiguousarray(f["x"].reshape(TB, P).T),
        "tok_W": np.ascontiguousarray(f["L0_tok_W"].T),
        "uv_w": np.concatenate([np.concatenate([f[A + "u_w"].T, f[A + "v_w"].T], 1), row(A + "u_b", A + "v_b")], 0),
        "rpe_w": row(A + "pos_w", A + "pos_b", A + "rpe_lw", A + "rpe_lb"),
        "kernel_w": np.concatenate([f[A + "out_w"].T, f[A + "out_w"].T, row(A + "out_b")], 0),
        "o_w": np.concatenate([f[A + "o_w"].T, row(A + "o_b")], 0),
        "pk_w": f["L0_ffn_Wq_pk"],
        "pk_keys": keys.reshape(P, 4 * 4 * NK),
        "kv_table": np.concatenate([f["L0_ffn_keys_table"], f["L0_ffn_values_table"]], 1),
        "q_w": f["L0_ffn_Wq"].reshape(D, H, D).transpose(1, 0, 2).reshape(H * D, D),
        "out_proj": out_proj.reshape(H * (D + 1), D + 1),
        "l1_w": l1_w.reshape(D, 2 * P),
        "router_w": f["L1_ffn_router_w"].T,
        "w1": np.concatenate([f["L1_ffn_w1"].transpose(1, 0, 2).reshape(D, E * D), row("L1_ffn_b1")], 0),
        "w2": w2.reshape(P, E // 2 * P),
        "b2": row("L1_ffn_b2"),
        "t_w": np.concatenate([f[A + "t_w"].T, row(A + "t_b")], 0),
    }
    return {k: np.ascontiguousarray(v) for k, v in d.items()}


def kernel(**inputs):
    import concourse.bacc as bacc
    from concourse.bass_utils import run_bass_kernel_spmd

    nc = bacc.Bacc("TRN2", target_bir_lowering=False, num_devices=1)
    arrays = {**data_layout({k: np.asarray(v) for k, v in inputs.items()}), **tower_constants()}
    handles = {k: nc.dram_tensor(f"in_{k}", v.shape, mybir.dt.from_np(v.dtype), kind="ExternalInput").ap()
               for k, v in arrays.items()}
    out = nc.dram_tensor("out_h", (T, D), F32, kind="ExternalOutput").ap()
    tower(nc, handles, out)
    result = run_bass_kernel_spmd(nc, [{f"in_{k}": v for k, v in arrays.items()}], core_ids=[0])
    return result.results[0]["out_h"].reshape(B, N, D)
```

```python
from contextlib import ExitStack

import numpy as np

import concourse.bass as bass
from concourse import mybir

F32 = mybir.dt.float32
F16 = mybir.dt.float16
BF16 = mybir.dt.bfloat16
I32 = mybir.dt.int32
U32 = mybir.dt.uint32
ALU = mybir.AluOpType
ACT = mybir.ActivationFunctionType
AX = mybir.AxisListType.X

P = 128
B, N, D = 4, 1024, 64
NB = N // P
T = B * N
TB = T // P
D1 = 192
RPE, LAYERS = 8, 3
FB = N // P
H = 8
DK = 32
NK = 64
TOPK = 16
RECTS = [(0, 1, 16), (1, 1, 8), (2, 2, 5), (4, 4, 3), (8, 8, 1)]
CAND = sum(na * nb for _, na, nb in RECTS)
E = 8
VOCAB = 4360
LN_EPS = 1e-5
RMS_EPS = 1e-8
LOWEST = -3.0e38
MASKED = -1.0e30


def tower_constants():
    j = np.arange(N)
    k = np.arange(N)
    turn = 2 * np.pi * ((j[:, None] * k[None, :]) % (2 * N)) / (2 * N)
    re, im = np.cos(turn), -np.sin(turn)
    im[:, 0] = (-1.0) ** j
    fwd = np.stack([re, im], 0).reshape(2, NB, P, FB, P)
    dft = np.ascontiguousarray(fwd.transpose(3, 2, 1, 0, 4).reshape(FB * P, NB * 2 * P)).astype(np.float32)
    gain = np.full(N, 2.0 / (2 * N))
    gain[0] = 1.0 / (2 * N)
    ire, iim = re * gain, im * gain
    inv = np.stack([ire, iim], 0).reshape(2, NB, P, FB, P)
    idft = np.ascontiguousarray(inv.transpose(1, 4, 3, 0, 2).reshape(NB * P, FB * 2 * P)).astype(np.float32)
    sign = np.ones((16, FB, 2, P), np.float32)
    odd = (k.reshape(FB, P) % 2) == 1
    sign[8:] = np.where(odd, -1.0, 1.0)[None, :, None, :]
    keep = np.ones((17, FB, P), np.float32)
    keep[:, 0, 0] = 0.0
    offset = np.zeros((1, FB, 2, P), np.float32)
    offset[0, 0, 0, 0] = 2 * N
    pos = np.concatenate([[0.0], np.arange(1, N), [0.0], -np.arange(1, N)[::-1]]).astype(np.float32)
    causal = np.where(np.arange(2 * N - P)[None, :] - (N - P) > np.arange(P)[:, None], MASKED, 0.0)
    return {
        "c_ident": np.eye(P, dtype=np.float32),
        "c_dft": dft,
        "c_idft": idft,
        "c_sign": sign.reshape(16, FB * 2 * P),
        "c_keep": keep.reshape(17, FB * P),
        "c_offset": offset.reshape(1, FB * 2 * P),
        "c_pos": np.ascontiguousarray(pos.reshape(2 * NB, P).T),
        "c_causal": causal.astype(np.float32),
        "c_rank": np.tile(np.arange(CAND, dtype=np.float32), (P, 1)),
        "c_head": np.tile(np.repeat(np.arange(H, dtype=np.float32) * NK * NK + NK * NK // 2, TOPK), (P, 1)),
        "c_expert": np.tile(np.arange(E, dtype=np.float32), (P, 1)),
    }


class Chain:

    def __init__(self, engine, semaphore):
        self.engine, self.semaphore, self.count = engine, semaphore, 0

    def mark(self, instruction):
        self.count += 1
        return instruction.then_inc(self.semaphore, 1)

    def wait(self):
        self.engine.wait_ge(self.semaphore, self.count)

    def link(self, instruction):
        self.mark(instruction)
        self.wait()

    def clear(self):
        self.wait()
        self.engine.sem_clear(self.semaphore)
        self.count = 0


def bc(ap, axis, n):
    shape = list(ap.shape)
    return ap.unsqueeze(axis).broadcast_to(shape[:axis] + [n] + shape[axis:])




class Mem:

    def __init__(self, nc, ctx, stage):
        self.nc, self.ctx, self.stage = nc, ctx, stage

    def sb(self, name, shape, dt=F32):
        return self.ctx.enter_context(self.nc.sbuf_tensor(f"{self.stage}_{name}", shape, dt))

    def ps(self, name, shape, dt=F32):
        return self.ctx.enter_context(self.nc.psum_tensor(f"{self.stage}_{name}", shape, dt))

    def sem(self, name):
        return self.ctx.enter_context(self.nc.semaphore(f"{self.stage}_{name}"))


def layernorm_a(dve, chain, x, xc, sq, stat):
    chain.link(dve.tensor_reduce(stat[:, 0, :], x, AX, ALU.add))
    chain.link(dve.tensor_scalar(stat[:, 1, :], stat[:, 0, :], -1.0 / D, None, ALU.mult))
    chain.link(dve.tensor_tensor(xc, x, bc(stat[:, 1, :], 2, D), ALU.add))
    chain.link(dve.tensor_tensor(sq, xc, xc, ALU.mult))
    chain.link(dve.tensor_reduce(stat[:, 2, :], sq, AX, ALU.add))
    chain.link(dve.tensor_scalar(stat[:, 2, :], stat[:, 2, :], 1.0 / D, LN_EPS, ALU.mult, ALU.add))


def flip_rows(pe, out, x, ident):
    pe.matmul(out[0:D, 0:P], x[:, 0, 0:D], ident[:, :], start=True, stop=True)
    for t in range(1, NB):
        last = pe.transpose(out[0:D, t * P:(t + 1) * P], x[:, t, 0:D], ident[:, :])
    return last


def embed_stage(nc, a, st):
    with ExitStack() as ctx:
        m = Mem(nc, ctx, "em")
        ids = m.sb("ids", [P, TB], I32)
        not_pad = m.sb("not_pad", [P, TB])
        ident = m.sb("ident", [P, P])
        uv_w = m.sb("uv_w", [D + 1, 2 * D1])
        rpe_w = m.sb("rpe_w", [P, 2 * RPE + LAYERS * (RPE * RPE + RPE)])
        pos = m.sb("pos", [P, 2 * NB])
        xc = m.sb("xc", [P, NB, D])
        sq = m.sb("sq", [P, NB, D])
        xn = m.sb("xn", [P, NB, D])
        stat = m.sb("stat", [P, 4, NB])
        xnT = m.sb("xnT", [D + 1, N])
        rh = m.sb("rh", [P, 2 * NB, RPE])
        rr = m.sb("rr", [P, 2 * NB, RPE])
        rprod = m.sb("rprod", [P, 2 * NB, RPE, RPE])
        rstat = m.sb("rstat", [P, 4, 2 * NB])
        xnT_ps = m.ps("xnT_ps", [D, N])
        uv_ps = m.ps("uv_ps", [P, 2, 512])

        loaded = m.sem("loaded")
        ids_in = m.sem("ids_in")
        embedded = m.sem("embedded")
        dve_steps = m.sem("dve_steps")
        act_steps = m.sem("act_steps")
        rpe_square = m.sem("rpe_square")
        rpe_root = m.sem("rpe_root")
        ln_var = m.sem("ln_var")
        ln_std = m.sem("ln_std")
        xn_ready = m.sem("xn_ready")
        xnT_ready = m.sem("xnT_ready")
        xnT_copied = m.sem("xnT_copied")
        uv_ready = m.sem("uv_ready")
        uv_taken = m.sem("uv_taken")
        ones_set = m.sem("ones_set")
        block = ctx.enter_context(nc.Block())

        @block.sync
        def _(sp):
            for semaphore in (xnT_ready, uv_ready, xnT_copied, uv_taken):
                sp.sem_inc(semaphore, 1)
            sp.dma_start(ids[:, :], a["ids"]).then_inc(ids_in, 16)
            sp.dma_start(rpe_w[:, :], a["rpe_w"].partition_broadcast(P)).then_inc(loaded, 16)
            sp.dma_start(pos[:, :], a["c_pos"]).then_inc(loaded, 16)
            sp.dma_start(ident[:, :], a["c_ident"]).then_inc(loaded, 16)
            sp.dma_start(uv_w[:, :], a["uv_w"]).then_inc(loaded, 16)

        @block.gpsimd
        def _(pool):
            pool.wait_ge(ids_in, 16)
            for t in range(TB):
                pool.indirect_dma_start(
                    st["h"][:, t, :], None, a["tok_W"],
                    bass.IndirectOffsetOnAxis(ids[:, t:t + 1].bitcast(U32), 0)).then_inc(embedded, 16)

        @block.vector
        def _(dve):
            chain = Chain(dve, dve_steps)
            dve.memset(xnT[D:D + 1, :], 1.0).then_inc(ones_set, 1)
            dve.wait_ge(ids_in, 16)
            chain.link(dve.tensor_scalar(not_pad[:, :], ids[:, :], 0.0, None, ALU.not_equal))
            dve.wait_ge(loaded, 64)
            w = rpe_w[:, :]
            chain.link(dve.tensor_tensor(rh[:, :, :], bc(pos[:, :], 2, RPE), bc(w[:, 0:RPE], 1, 2 * NB), ALU.mult))
            chain.link(dve.tensor_tensor(rh[:, :, :], rh[:, :, :], bc(w[:, RPE:2 * RPE], 1, 2 * NB), ALU.add))
            for layer in range(LAYERS + 1):
                chain.link(dve.tensor_tensor(rr[:, :, :], rh[:, :, :], rh[:, :, :], ALU.mult))
                chain.link(dve.tensor_reduce(rstat[:, 0, :], rr[:, :, :], AX, ALU.add))
                dve.tensor_scalar(rstat[:, 1, :], rstat[:, 0, :], 1.0 / RPE, None, ALU.mult).then_inc(rpe_square, 1)
                dve.wait_ge(rpe_root, layer + 1)
                chain.link(dve.tensor_scalar(rstat[:, 3, :], rstat[:, 2, :], RMS_EPS, None, ALU.add))
                chain.link(dve.reciprocal(rstat[:, 0, :], rstat[:, 3, :]))
                chain.link(dve.tensor_tensor(rr[:, :, :], rh[:, :, :], bc(rstat[:, 0, :], 2, RPE), ALU.mult))
                if layer == LAYERS:
                    out = st["rpe"][:, :, :, :].rearrange("p t s c -> p s t c")
                    src = rr[:, :, :].rearrange("p (s t) c -> p s t c", s=2)
                    chain.link(dve.tensor_scalar(out[:, 0], src[:, 0], 0.0, None, ALU.max))
                    chain.link(dve.tensor_scalar(out[:, 1], src[:, 1], 0.0, None, ALU.max))
                    continue
                chain.link(dve.tensor_scalar(rr[:, :, :], rr[:, :, :], 0.0, None, ALU.max))
                at = 2 * RPE + layer * RPE * RPE
                wl = w[:, at:at + RPE * RPE].rearrange("p (o c) -> p o c", c=RPE)
                for o in range(RPE):
                    chain.mark(dve.tensor_tensor(rprod[:, :, o, :], rr[:, :, :], bc(wl[:, o, :], 1, 2 * NB), ALU.mult))
                chain.wait()
                chain.link(dve.tensor_reduce(rh[:, :, :], rprod[:, :, :, :], AX, ALU.add))
                at = 2 * RPE + LAYERS * RPE * RPE + layer * RPE
                chain.link(dve.tensor_tensor(rh[:, :, :], rh[:, :, :], bc(w[:, at:at + RPE], 1, 2 * NB), ALU.add))
            dve.wait_ge(embedded, 16 * TB)
            chain.link(dve.tensor_tensor(st["h"][:, :, :], st["h"][:, :, :], bc(not_pad[:, :], 2, D), ALU.mult))
            chain.clear()
            with dve.Fori(0, B) as b:
                layernorm_a(dve, chain, st["h"][:, bass.ds(b * NB, NB), :], xc[:, :, :], sq[:, :, :], stat)
                chain.link(dve.tensor_copy(stat[:, 1, :], stat[:, 2, :]))
                dve.tensor_copy(stat[:, 0, :], stat[:, 2, :]).then_inc(ln_var, 1)
                dve.wait_ge(ln_std, b + 1)
                chain.link(dve.reciprocal(stat[:, 1, :], stat[:, 3, :]))
                dve.wait_ge(xnT_ready, b + 1)
                chain.link(dve.tensor_tensor(xn[:, :, :], xc[:, :, :], bc(stat[:, 1, :], 2, D), ALU.mult))
                dve.tensor_copy(st["xn"][:, bass.ds(b * NB, NB), :], xn[:, :, :]).then_inc(xn_ready, 1)
                chain.clear()

        @block.scalar
        def _(act):
            chain = Chain(act, act_steps)
            for layer in range(LAYERS + 1):
                act.wait_ge(rpe_square, layer + 1)
                act.activation(rstat[:, 2, :], rstat[:, 1, :], ACT.Sqrt).then_inc(rpe_root, 1)
            with act.Fori(0, B) as b:
                act.wait_ge(ln_var, b + 1)
                act.activation(stat[:, 3, :], stat[:, 0, :], ACT.Sqrt).then_inc(ln_std, 1)
                act.wait_ge(xnT_ready, b + 2)
                act.wait_ge(uv_ready, b * NB + 1)
                act.activation(xnT[0:D, :], xnT_ps[:, :], ACT.Copy).then_inc(xnT_copied, 1)
                chain.link(act.activation(st["xnT"][:, bass.ds(b * N, N)], xnT_ps[:, :], ACT.Copy))
                for t in range(NB):
                    act.wait_ge(uv_ready, b * NB + t + 2)
                    act.activation(st["u"][:, bass.ds(b * NB + t, 1), :], uv_ps[:, t % 2, 0:D1], ACT.Silu)\
                       .then_inc(act_steps, 1)
                    act.activation(st["v"][:, t, bass.ds(b, 1), :], uv_ps[:, t % 2, D1:2 * D1], ACT.Silu)\
                       .then_inc(uv_taken, 1)
                chain.count += NB
                chain.clear()

        @block.tensor
        def _(pe):
            pe.wait_ge(loaded, 64)
            pe.wait_ge(ones_set, 1)
            with pe.Fori(0, B) as b:
                pe.wait_ge(xn_ready, b + 1)
                pe.wait_ge(xnT_copied, b + 1)
                pe.wait_ge(uv_taken, b * NB + 1)
                flip_rows(pe, xnT_ps, xn, ident).then_inc(xnT_ready, 1)
                pe.wait_ge(xnT_copied, b + 2)
                for t in range(NB):
                    if t >= 2:
                        pe.wait_ge(uv_taken, b * NB + t)
                    pe.matmul(uv_ps[:, t % 2, 0:2 * D1], xnT[:, t * P:(t + 1) * P], uv_w[:, :],
                              start=True, stop=True).then_inc(uv_ready, 1)


def conv_stage(nc, a, st):
    HALF = B * D1 // 2
    with ExitStack() as ctx:
        m = Mem(nc, ctx, "cv")
        sign = m.sb("sign", [16, FB * 2 * P])
        keep = m.sb("keep", [17, FB * P])
        kernel_w = m.sb("kernel_w", [17, D1])
        table = [m.sb(f"table{i}", [P, NB * 2 * P]) for i in range(2)]
        spec8 = m.sb("spec8", [17, 2 * P])
        spec3 = m.sb("spec3", [17, 3, P])
        temp = m.sb("temp", [17, 2, P])
        ker = m.sb("ker", [P, 3, D1])
        v_re = m.sb("v_re", [P, B, D1])
        v_im = m.sb("v_im", [P, B, D1])
        prod = m.sb("prod", [P, 4, B, D1])
        out_f = m.sb("out_f", [P, 2 * FB, B * D1])
        spec8_ps = m.ps("spec8_ps", [16, 512])
        ker_ps = m.ps("ker_ps", [P, 2, 512])
        v_ps = m.ps("v_ps", [P, 4, 512])

        loaded = m.sem("loaded")
        table_in = [m.sem(f"table_in{i}") for i in range(2)]
        offset_in = m.sem("offset_in")
        dve_steps = m.sem("dve_steps")
        spec8_ready = m.sem("spec8_ready")
        spec3_ready = m.sem("spec3_ready")
        ker_ready = m.sem("ker_ready")
        ker_copied = m.sem("ker_copied")
        v_ready = m.sem("v_ready")
        v_copied = m.sem("v_copied")
        product_done = m.sem("product_done")
        y_ready = m.sem("y_ready")
        y_copied = m.sem("y_copied")
        block = ctx.enter_context(nc.Block())

        @block.sync
        def _(sp):
            for semaphore in (spec3_ready, v_copied, ker_copied, product_done, ker_ready):
                sp.sem_inc(semaphore, 1)
            for semaphore in (v_ready, y_ready, y_copied):
                sp.sem_inc(semaphore, 2)
            sp.dma_start(sign[:, :], a["c_sign"]).then_inc(loaded, 16)
            sp.dma_start(keep[:, :], a["c_keep"]).then_inc(loaded, 16)
            sp.dma_start(kernel_w[:, :], a["kernel_w"]).then_inc(loaded, 16)
            with sp.Fori(0, FB // 2) as f:
                for i in range(2):
                    src = a["c_dft"][bass.ds(f * (2 * P) + i * P, P), :]
                    sp.wait_ge(v_ready, f * 2 + i + 1)
                    sp.dma_start(table[i][:, :], src).then_inc(table_in[i], 16)
                    off = a["c_offset"][:, bass.ds(f * (4 * P) + i * 2 * P, 2 * P)]
                    sp.wait_ge(spec3_ready, f * 2 + i + 1)
                    sp.dma_start(spec8[16:17, :], off).then_inc(offset_in, 16)
            sp.wait_ge(v_ready, FB + 2)
            with sp.Fori(0, NB // 2) as t:
                for i in range(2):
                    src = a["c_idft"][bass.ds(t * (2 * P) + i * P, P), :]
                    sp.wait_ge(y_ready, t * 2 + i + 1)
                    sp.dma_start(table[i][:, :], src).then_inc(table_in[i], 16)

        @block.tensor
        def _(pe):
            pe.wait_ge(loaded, 48)
            with pe.Fori(0, FB // 2) as f:
                for i in range(2):
                    k = f * 2 + i
                    tab = table[i][:, :].rearrange("p (t c) -> p t c", t=NB)
                    pe.wait_ge(spec3_ready, k + 1)
                    pe.wait_ge(table_in[i], f * 16 + 16)
                    for t in range(NB):
                        last = pe.matmul(spec8_ps[:, 0:2 * P], st["rpe"][:, t, :, :].rearrange("p s c -> p (s c)"),
                                         tab[:, t, :], start=(t == 0), stop=(t == NB - 1))
                    last.then_inc(spec8_ready, 1)
                    pe.wait_ge(v_copied, k + 1)
                    for half in range(2):
                        for part in range(2):
                            for t in range(NB):
                                last = pe.matmul(v_ps[:, 2 * part + half, 0:HALF], tab[:, t, part * P:(part + 1) * P],
                                                 st["v"][:, t, 2 * half:2 * half + 2, :].rearrange("p b c -> p (b c)"),
                                                 start=(t == 0), stop=(t == NB - 1))
                    last.then_inc(v_ready, 1)
                    pe.wait_ge(ker_copied, k + 1)
                    pe.wait_ge(spec3_ready, k + 2)
                    for part in range(3):
                        last = pe.matmul(ker_ps[:, part // 2, (part % 2) * D1:(part % 2 + 1) * D1], spec3[:, part, :],
                                         kernel_w[:, :], start=(part != 1), stop=(part != 0),
                                         skip_group_check=True)
                    last.then_inc(ker_ready, 1)
            pe.wait_ge(product_done, FB + 1)
            pe.wait_ge(v_copied, FB + 1)
            with pe.Fori(0, NB // 2) as t:
                for i in range(2):
                    tab = table[i][:, :].rearrange("p (f j) -> p f j", f=2 * FB)
                    pe.wait_ge(y_copied, t * 2 + i + 1)
                    pe.wait_ge(table_in[i], t * 16 + 16 + 16 * (FB // 2))
                    for half in range(2):
                        for f in range(2 * FB):
                            last = pe.matmul(v_ps[:, 2 * i + half, 0:HALF], tab[:, f, :],
                                             out_f[:, f, half * HALF:(half + 1) * HALF],
                                             start=(f == 0), stop=(f == 2 * FB - 1))
                    last.then_inc(y_ready, 1)

        @block.scalar
        def _(act):
            with act.Fori(0, FB) as k:
                act.wait_ge(product_done, k + 1)
                act.wait_ge(v_ready, k + 3)
                act.activation(v_re[:, :, :].rearrange("p (h b) c -> p h (b c)", h=2), v_ps[:, 0:2, 0:HALF], ACT.Copy)
                act.activation(v_im[:, :, :].rearrange("p (h b) c -> p h (b c)", h=2), v_ps[:, 2:4, 0:HALF],
                               ACT.Copy).then_inc(v_copied, 1)
                act.wait_ge(ker_ready, k + 2)
                act.activation(ker[:, 0:2, :], ker_ps[:, 0, 0:2 * D1].rearrange("p (r c) -> p r c", r=2), ACT.Copy)
                act.activation(ker[:, 2, :], ker_ps[:, 1, 0:D1], ACT.Copy).then_inc(ker_copied, 1)
            with act.Fori(0, NB // 2) as t:
                for i in range(2):
                    act.wait_ge(y_ready, t * 2 + i + 3)
                    act.activation(st["y"][:, bass.ds(t * 2 + i, 1), :].rearrange("p o (h c) -> p (o h) c", h=2),
                                   v_ps[:, 2 * i:2 * i + 2, 0:HALF], ACT.Copy).then_inc(y_copied, 1)

        @block.vector
        def _(dve):
            chain = Chain(dve, dve_steps)
            dve.wait_ge(loaded, 48)
            with dve.Fori(0, FB) as k:
                dve.wait_ge(offset_in, k * 16 + 16)
                dve.wait_ge(spec8_ready, k + 1)
                chain.link(dve.tensor_tensor(spec8[0:16, :], spec8_ps[:, 0:2 * P], sign[:, bass.ds(k * (2 * P), 2 * P)],
                                             ALU.mult))
                kp = keep[:, bass.ds(k * P, P)]
                dve.wait_ge(ker_ready, k + 1)
                chain.mark(dve.tensor_copy(spec3[:, 0, :], spec8[:, 0:P]))
                chain.mark(dve.tensor_tensor(spec3[:, 1, :], spec8[:, P:2 * P], kp, ALU.mult))
                chain.link(dve.tensor_tensor(temp[:, 0, :], spec8[:, 0:P], kp, ALU.mult))
                chain.link(dve.tensor_tensor(temp[:, 1, :], spec8[:, P:2 * P], spec3[:, 1, :], ALU.subtract))
                chain.link(dve.tensor_tensor(spec3[:, 2, :], temp[:, 0, :], temp[:, 1, :], ALU.add))
                dve.sem_inc(spec3_ready, 1)
                dve.wait_ge(v_copied, k + 2)
                dve.wait_ge(ker_copied, k + 2)
                k_re, k_im, k_re2 = (bc(ker[:, i, :], 1, B) for i in range(3))
                chain.mark(dve.tensor_tensor(prod[:, 0], v_re[:, :, :], k_re, ALU.mult))
                chain.mark(dve.tensor_tensor(prod[:, 1], v_im[:, :, :], k_im, ALU.mult))
                chain.mark(dve.tensor_tensor(prod[:, 2], v_im[:, :, :], k_re2, ALU.mult))
                chain.link(dve.tensor_tensor(prod[:, 3], v_re[:, :, :], k_im, ALU.mult))
                flat = prod[:, :, :, :].rearrange("p q b c -> p q (b c)")
                chain.mark(dve.tensor_tensor(out_f[:, bass.ds(k * 2, 1), :], flat[:, 0:1], flat[:, 1:2], ALU.subtract))
                chain.link(dve.tensor_tensor(out_f[:, bass.ds(k * 2 + 1, 1), :], flat[:, 2:3], flat[:, 3:4], ALU.add))
                dve.sem_inc(product_done, 1)
                chain.clear()


def gate_stage(nc, a, st):
    with ExitStack() as ctx:
        m = Mem(nc, ctx, "gt")
        ident = m.sb("ident", [P, P])
        o_w1 = m.sb("o_w1", [P, D])
        o_w2 = m.sb("o_w2", [D1 - P + 1, D])
        t_w = m.sb("t_w", [D + 1, D])
        uy = m.sb("uy", [P, NB, D1])
        uyT1 = m.sb("uyT1", [P, N])
        uyT2 = m.sb("uyT2", [D1 - P + 1, N])
        dT = m.sb("dT", [D + 1, N])
        z = m.sb("z", [P, NB, D])
        sq = m.sb("sq", [P, NB, D])
        zn = m.sb("zn", [P, NB, D])
        xr = m.sb("xr", [P, NB, D])
        h1 = m.sb("h1", [P, NB, D])
        xc = m.sb("xc", [P, NB, D])
        xn = m.sb("xn", [P, NB, D])
        stat = m.sb("stat", [P, 4, NB])
        rms = m.sb("rms", [P, 4, NB])
        uyT1_ps = m.ps("uyT1_ps", [P, N])
        uyT2_ps = m.ps("uyT2_ps", [D1 - P, N])
        outT_ps = m.ps("outT_ps", [D, N])
        z_ps = m.ps("z_ps", [P, NB, D])

        loaded = m.sem("loaded")
        ones_set = m.sem("ones_set")
        dve_steps = m.sem("dve_steps")
        act_steps = m.sem("act_steps")
        uy_ready = m.sem("uy_ready")
        uyT_ready = m.sem("uyT_ready")
        uyT_copied = m.sem("uyT_copied")
        outT_ready = m.sem("outT_ready")
        dT_ready = m.sem("dT_ready")
        z_ready = m.sem("z_ready")
        square_ready = m.sem("square_ready")
        root_ready = m.sem("root_ready")
        zn_ready = m.sem("zn_ready")
        xr_ready = m.sem("xr_ready")
        ln_var = m.sem("ln_var")
        ln_std = m.sem("ln_std")
        xn_ready = m.sem("xn_ready")
        xnT_ready = m.sem("xnT_ready")
        xnT_copied = m.sem("xnT_copied")
        xnT_stored = m.sem("xnT_stored")
        block = ctx.enter_context(nc.Block())

        @block.sync
        def _(sp):
            for semaphore in (xnT_copied, uyT_ready, xnT_ready):
                sp.sem_inc(semaphore, 1)
            sp.dma_start(ident[:, :], a["c_ident"]).then_inc(loaded, 16)
            sp.dma_start(o_w1[:, :], a["o_w"][0:P, :]).then_inc(loaded, 16)
            sp.dma_start(o_w2[:, :], a["o_w"][P:D1 + 1, :]).then_inc(loaded, 16)
            sp.dma_start(t_w[:, :], a["t_w"]).then_inc(loaded, 16)
            sp.wait_ge(xnT_copied, B + 1)
            sp.dma_start(st["xnT_d"][:, 0:T], st["xnT"][:, :]).then_inc(xnT_stored, 16)
            sp.dma_start(st["xnT_d"][:, T:T + P], st["xnT"][:, 0:P]).then_inc(xnT_stored, 16)
            sp.wait_ge(xnT_stored, 32)

        @block.tensor
        def _(pe):
            pe.wait_ge(loaded, 64)
            pe.wait_ge(ones_set, 2)
            with pe.Fori(0, B) as b:
                pe.wait_ge(uy_ready, b + 1)
                for t in range(NB):
                    pe.transpose(uyT1_ps[:, t * P:(t + 1) * P], uy[:, t, 0:P], ident[:, :])
                    last = pe.transpose(uyT2_ps[:, t * P:(t + 1) * P], uy[:, t, P:D1], ident[:, :])
                last.then_inc(uyT_ready, 1)
                pe.wait_ge(uyT_copied, b + 1)
                pe.wait_ge(xnT_copied, b + 1)
                for half in range(2):
                    c = slice(half * 512, half * 512 + 512)
                    pe.matmul(outT_ps[:, c], o_w1[:, :], uyT1[:, c], start=True, stop=False)
                    last = pe.matmul(outT_ps[:, c], o_w2[:, :], uyT2[:, c], start=False, stop=True)
                last.then_inc(outT_ready, 1)
                pe.wait_ge(dT_ready, b + 1)
                for t in range(NB):
                    last = pe.matmul(z_ps[:, t, :], dT[:, t * P:(t + 1) * P], t_w[:, :], start=True, stop=True)
                last.then_inc(z_ready, 1)
                pe.wait_ge(xn_ready, b + 1)
                flip_rows(pe, outT_ps, xn, ident).then_inc(xnT_ready, 1)

        @block.scalar
        def _(act):
            chain = Chain(act, act_steps)
            with act.Fori(0, B) as b:
                act.wait_ge(uyT_ready, b + 2)
                chain.mark(act.activation(uyT1[:, :], uyT1_ps[:, :], ACT.Copy))
                chain.link(act.activation(uyT2[0:D1 - P, :], uyT2_ps[:, :], ACT.Copy))
                act.sem_inc(uyT_copied, 1)
                act.wait_ge(square_ready, b + 1)
                act.activation(rms[:, 1, :], rms[:, 0, :], ACT.Sqrt).then_inc(root_ready, 1)
                act.wait_ge(zn_ready, b + 1)
                act.activation(xr[:, :, :], zn[:, :, :], ACT.Silu).then_inc(xr_ready, 1)
                act.wait_ge(ln_var, b + 1)
                act.activation(stat[:, 3, :], stat[:, 0, :], ACT.Sqrt).then_inc(ln_std, 1)
                act.wait_ge(xnT_ready, b + 2)
                act.activation(st["xnT"][:, bass.ds(b * N, N)], outT_ps[:, :], ACT.Copy).then_inc(xnT_copied, 1)
                chain.clear()

        @block.vector
        def _(dve):
            chain = Chain(dve, dve_steps)
            dve.memset(uyT2[D:D + 1, :], 1.0).then_inc(ones_set, 1)
            dve.memset(dT[D:D + 1, :], 1.0).then_inc(ones_set, 1)
            with dve.Fori(0, B) as b:
                blocks = bass.ds(b * NB, NB)
                dve.wait_ge(uyT_ready, b + 1)
                dve.tensor_tensor(uy[:, :, :], st["u"][:, blocks, :], st["y"][:, :, bass.ds(b * D1, D1)], ALU.mult)\
                   .then_inc(uy_ready, 1)
                dve.wait_ge(outT_ready, b + 1)
                dve.tensor_tensor(dT[0:D, :], st["xnT"][:, bass.ds(b * N, N)], outT_ps[:, :], ALU.subtract)\
                   .then_inc(dT_ready, 1)
                dve.wait_ge(z_ready, b + 1)
                chain.link(dve.tensor_copy(z[:, :, :], z_ps[:, :, :]))
                chain.link(dve.tensor_tensor(sq[:, :, :], z[:, :, :], z[:, :, :], ALU.mult))
                chain.link(dve.tensor_reduce(rms[:, 2, :], sq[:, :, :], AX, ALU.add))
                dve.tensor_scalar(rms[:, 0, :], rms[:, 2, :], 1.0 / D1, None, ALU.mult).then_inc(square_ready, 1)
                dve.wait_ge(root_ready, b + 1)
                chain.link(dve.tensor_scalar(rms[:, 2, :], rms[:, 1, :], RMS_EPS, None, ALU.add))
                chain.link(dve.reciprocal(rms[:, 3, :], rms[:, 2, :]))
                dve.tensor_tensor(zn[:, :, :], z[:, :, :], bc(rms[:, 3, :], 2, D), ALU.mult).then_inc(zn_ready, 1)
                chain.link(dve.tensor_tensor(h1[:, :, :], st["h"][:, blocks, :], st["xn"][:, blocks, :], ALU.add))
                dve.wait_ge(xr_ready, b + 1)
                chain.link(dve.tensor_tensor(xc[:, :, :], h1[:, :, :], xr[:, :, :], ALU.add))
                chain.link(dve.tensor_copy(st["h"][:, blocks, :], xc[:, :, :]))
                layernorm_a(dve, chain, xc[:, :, :], h1[:, :, :], sq[:, :, :], stat)
                dve.tensor_copy(stat[:, 0, :], stat[:, 2, :]).then_inc(ln_var, 1)
                dve.wait_ge(ln_std, b + 1)
                chain.link(dve.reciprocal(stat[:, 1, :], stat[:, 3, :]))
                dve.wait_ge(xnT_ready, b + 1)
                chain.link(dve.tensor_tensor(xn[:, :, :], h1[:, :, :], bc(stat[:, 1, :], 2, D), ALU.mult))
                dve.sem_inc(xn_ready, 1)
                chain.link(dve.tensor_copy(st["xn"][:, blocks, :], xn[:, :, :]))
                chain.clear()


RING = 4
HALF_N = N // 2
ATTN_SCALE = float(D) ** -0.5


def mixer_stage(nc, a, st, out):
    with ExitStack() as ctx:
        m = Mem(nc, ctx, "mx")
        xnT = st["xnT_d"]
        ident = m.sb("ident", [P, P])
        ident_b = m.sb("ident_b", [P, P], BF16)
        causal = m.sb("causal", [P, 2 * N - P], BF16)
        pk_w = m.sb("pk_w", [D, 4 * P])
        keys = m.sb("keys", [P, 4, 4 * NK])
        rank = m.sb("rank", [P, CAND])
        rank_h = m.sb("rank_h", [P, CAND], F16)
        head_base = m.sb("head_base", [P, H, TOPK])
        expert_id = m.sb("expert_id", [P, E])
        q_w = m.sb("q_w", [D, H * D])
        o_w = m.sb("o_w", [P, H // 2, D])
        l1_w = m.sb("l1_w", [D, 2, P])
        router = m.sb("router", [D, E])
        w1 = m.sb("w1", [D + 1, E * D])
        w2 = m.sb("w2", [P, E // 2, P])
        b2 = m.sb("b2", [1, E * D])
        ones = m.sb("ones", [1, P])
        xb = m.sb("xb", [D, P])
        qT_pk = m.sb("qT_pk", [P, 4, P])
        S = m.sb("S", [P, 2 * H, NK])
        S2 = m.sb("S2", [P, 2 * H, NK])
        V = m.sb("V", [P, 2 * H, TOPK])
        I = m.sb("I", [P, 2 * H, TOPK], U32)
        If = m.sb("If", [P, 2 * H, TOPK])
        C = m.sb("C", [P, H, CAND])
        C2 = S2[:, :, :].rearrange("p a k -> p (a k)")[:, 0:H * CAND].rearrange("p (h c) -> p h c", c=CAND)
        hot = S[:, :, :].rearrange("p a k -> p (a k)").bitcast(F16)[:, 0:TOPK * CAND]\
            .rearrange("p (r c) -> p r c", c=CAND)
        CI = m.sb("CI", [P, H, CAND], F16)
        FV = m.sb("FV", [P, H, TOPK])
        FI = m.sb("FI", [P, H, TOPK], U32)
        FIf = m.sb("FIf", [P, H, TOPK], F16)
        row = m.sb("row", [P, H, TOPK])
        e_in = m.sb("e_in", [P, H, TOPK])
        e_out = m.sb("e_out", [P, H, TOPK])
        e_sum = m.sb("e_sum", [P, 2, H])
        next_w = m.sb("next_w", [P, H, TOPK])
        next_i = m.sb("next_i", [P, H, TOPK], U32)
        slot_w = m.sb("slot_w", [P, H, TOPK])
        slot_i = m.sb("slot_i", [P, H, TOPK], U32)
        G = m.sb("G", [P, H, TOPK, 2 * D])
        k_new = m.sb("k_new", [P, 2, D])
        KT = m.sb("KT", [D, H, N])
        VV = m.sb("VV", [P, NB, H, D + 1])
        xa = m.sb("xa", [D, P])
        qT = m.sb("qT", [D, 2, P])
        minus_max = m.sb("minus_max", [P, 2])
        row_max = m.sb("row_max", [P, 2])
        prob = m.sb("prob", [P, N])
        probT = m.sb("probT", [P, N])
        rz = m.sb("rz", [P, 2])
        o_all = m.sb("o_all", [P, H, D])
        oT_all = m.sb("oT_all", [P, H // 2, P])
        xc = m.sb("xc", [P, NB, D])
        sq = m.sb("sq", [P, NB, D])
        stat = m.sb("stat", [P, 4, NB])
        x3 = m.sb("x3", [P, NB, D + 1])
        x4 = m.sb("x4", [P, NB, D])
        xT = m.sb("xT", [D + 1, N])
        kT1 = m.sb("kT1", [D, N])
        qT1 = m.sb("qT1", [D, N])
        lg = m.sb("lg", [P, NB, E])
        pr = m.sb("pr", [P, NB, E])
        pv = m.sb("pv", [P, NB, E])
        pi = m.sb("pi", [P, NB, E], U32)
        pif = m.sb("pif", [P, NB, E])
        comb = m.sb("comb", [P, 2, NB, E])
        gate = m.sb("gate", [P, NB, E])
        r8 = m.sb("r8", [P, 2, NB])
        hT = [t[:, i * HALF_N:(i + 1) * HALF_N] for t in (prob, probT) for i in range(2)]
        yw = xc
        out_sb = m.sb("out_sb", [P, NB, D])
        sim_ps = m.ps("sim_ps", [P, 2 * H, NK])
        ring = m.ps("ring", [P, RING, 512])
        mix_ps = m.ps("mix_ps", [P, 2, 512])

        loaded = m.sem("loaded")
        T_loaded = m.sem("T_loaded")
        consts_set = m.sem("consts_set")
        dve_steps = m.sem("dve_steps")
        xb_in = m.sem("xb_in")
        q_ready = m.sem("q_ready")
        q_copied = m.sem("q_copied")
        sim_ready = m.sem("sim_ready")
        sim_taken = m.sem("sim_taken")
        e_in_ready = m.sem("e_in_ready")
        e_out_ready = m.sem("e_out_ready")
        slot_ready = m.sem("slot_ready")
        slot_seen = m.sem("slot_seen")
        gathered = [m.sem(f"gathered{h}") for h in range(H)]
        xa_in = m.sem("xa_in")
        kv_ready = m.sem("kv_ready")
        kq_ready = m.sem("kq_ready")
        kq_copied = m.sem("kq_copied")
        s_ready = m.sem("s_ready")
        max_ready = m.sem("max_ready")
        p_ready = m.sem("p_ready")
        pT_ready = m.sem("pT_ready")
        pT_copied = m.sem("pT_copied")
        o_ready = m.sem("o_ready")
        o_taken = m.sem("o_taken")
        heads_ready = m.sem("heads_ready")
        headsT_ready = m.sem("headsT_ready")
        headsT_copied = m.sem("headsT_copied")
        proj_ready = m.sem("proj_ready")
        proj_taken = m.sem("proj_taken")
        ln_var = m.sem("ln_var")
        ln_std = m.sem("ln_std")
        rows_ready = m.sem("rows_ready")
        l1_ready = m.sem("l1_ready")
        l1_copied = m.sem("l1_copied")
        logits_ready = m.sem("logits_ready")
        route_in = m.sem("route_in")
        route_out = m.sem("route_out")
        hid_ready = m.sem("hid_ready")
        hid_taken = m.sem("hid_taken")
        y_ready = m.sem("y_ready")
        y_taken = m.sem("y_taken")
        out_ready = m.sem("out_ready")
        out_stored = m.sem("out_stored")
        block = ctx.enter_context(nc.Block())
        T_LOADS, N_LOADS = 4, 10
        PIECES = 6
        GROUPS = tuple(((piece,), (piece + 1, piece + 2)) for piece in range(PIECES - 1)) + (((PIECES - 1,), (PIECES, NB)),)

        def cores(b, steps, pieces):
            return steps * H + (b - 1) * NB + min(max(pieces - 1, 0), 2) * (NB // 2)

        def schedule(engine, step, F):
            with engine.Fori(1, NB) as g:
                step(g, g - 1, (g - 1) * H)
            with engine.Fori(1, B) as b:
                step(b * NB, NB - 1, cores(b, b * NB - 1, 0))
                for pieces, (first, end) in GROUPS:
                    for piece in pieces:
                        F(b - 1, piece, b * NB + (first - 1), cores(b, b * NB + (first - 1), piece))
                    for s in range(first, end):
                        step(b * NB + s, s - 1, cores(b, b * NB + s - 1, pieces[-1] + 1))

        @block.sync
        def _(sp):
            for semaphore in (sim_taken, sim_ready, q_ready, kq_ready, out_stored, proj_taken, o_taken):
                sp.sem_inc(semaphore, 1)
            def load_xb(g):
                src = xnT[:, bass.ds(g * P, P)]
                sp.wait_ge(q_ready, g + 1)
                sp.dma_start(xb[:, :], src).then_inc(xb_in, 16)

            load_xb(0)
            for dst, src in (
                (pk_w[:, :], a["pk_w"]), (keys[:, :, :], a["pk_keys"].rearrange("p (c k) -> p c k", c=4)),
                (rank[:, :], a["c_rank"]), (head_base[:, :, :], a["c_head"].rearrange("p (h r) -> p h r", h=H)),
            ):
                sp.dma_start(dst, src).then_inc(T_loaded, 16)
            for dst, src in (
                (ident[:, :], a["c_ident"]), (G[:, 0, 0:2 * NB - 1, :].rearrange("p r d -> p (r d)"), a["c_causal"]),
                (expert_id[:, :], a["c_expert"]), (l1_w[:, :, :], a["l1_w"].rearrange("p (c k) -> p c k", c=2)),
                (router[:, :], a["router_w"]), (w1[:, :], a["w1"]),
                (w2[:, :, :], a["w2"].rearrange("p (c k) -> p c k", c=E // 2)), (b2[:, :], a["b2"]),
                (q_w[:, :], a["q_w"]), (o_w[:, :, :], a["out_proj"].rearrange("(c p) d -> p c d", p=P)),
            ):
                sp.dma_start(dst, src).then_inc(loaded, 16)

            def load_xa(g):
                src = xnT[:, bass.ds(g * P - P, P)]
                sp.wait_ge(kq_ready, g * H + (1 - H))
                sp.dma_start(xa[:, :], src).then_inc(xa_in, 16)

            def store_out(b):
                dst = out[bass.ds(b * N, N), :].rearrange("(t p) d -> p t d", p=P)
                sp.wait_ge(out_ready, b + 1)
                sp.dma_start(dst, out_sb[:, :, :]).then_inc(out_stored, 16)

            def load_blocks(g):
                load_xa(g)
                load_xb(g + 1)

            load_xb(1)
            with sp.Fori(1, NB) as g:
                load_blocks(g)
            with sp.Fori(1, B) as b:
                with sp.Fori(0, NB) as s:
                    load_blocks(b * NB + s)
                store_out(b - 1)
            load_xa(TB)
            store_out(B - 1)
            sp.wait_ge(out_stored, 16 * B + 1)

        @block.gpsimd
        def _(pool):
            with pool.Fori(0, TB) as g:
                for h in range(H):
                    pool.wait_ge(slot_ready, g * H + h + 1)
                    pool.sem_inc(slot_seen, 1)
                    for r in range(TOPK):
                        pool.indirect_dma_start(G[:, h, r, :], None, a["kv_table"],
                                                bass.IndirectOffsetOnAxis(slot_i[:, h, r:r + 1], 0))\
                            .then_inc(gathered[h], 16)

        @block.tensor
        def _(pe):
            pe.wait_ge(T_loaded, 16 * T_LOADS)

            def T(g):
                pe.wait_ge(sim_taken, g + 1)
                pe.wait_ge(xb_in, g * 16 + 16)
                for c in range(4):
                    last = pe.matmul(sim_ps[:, 2 * c:2 * c + 2, :].rearrange("p a k -> p (a k)"),
                                     pk_w[:, c * P:(c + 1) * P], xb[:, :], start=True, stop=True)
                last.then_inc(q_ready, 1)
                pe.wait_ge(q_copied, g + 1)
                for c in range(4):
                    last = pe.matmul(sim_ps[:, 4 * c:4 * c + 4, :].rearrange("p a k -> p (a k)"), qT_pk[:, c, :],
                                     keys[:, c, :], start=True, stop=True)
                last.then_inc(sim_ready, 1)

            def scores(queries, keysT, mask_at=None):
                for half in range(2):
                    last = pe.matmul(ring[:, half, :], queries, keysT[:, half * HALF_N:(half + 1) * HALF_N],
                                     start=True, stop=mask_at is None, skip_group_check=True)
                if mask_at is not None:
                    for half in range(2):
                        last = pe.matmul(ring[:, half, :], ident_b[:, :],
                                         causal[:, bass.ds(mask_at + half * HALF_N, HALF_N)],
                                         start=False, stop=True, skip_group_check=True)
                last.then_inc(s_ready, 1)

            def flip_probs(n):
                pe.wait_ge(p_ready, n + 1)
                for j in range(NB):
                    last = pe.transpose(ring[:, 2 + j // 4, (j % 4) * P:(j % 4 + 1) * P],
                                        prob[:, j * P:(j + 1) * P], ident[:, :])
                last.then_inc(pT_ready, 1)

            def weigh(n, values):
                pe.wait_ge(o_taken, n + 1)
                pe.wait_ge(pT_copied, n + 1)
                for j in range(NB):
                    last = pe.matmul(mix_ps[:, 1, 0:D + 1], probT[:, j * P:(j + 1) * P], values(j),
                                     start=(j == 0), stop=(j == NB - 1))
                last.then_inc(o_ready, 1)

            def step(g, place, base, more=True):
                if more:
                    T(g + 1)
                pe.wait_ge(xa_in, g * 16)

                def keys_and_queries(h):
                    pe.wait_ge(kv_ready, (g - 1) * H + h + 1)
                    pe.matmul(mix_ps[0:D, 0, 0:P], k_new[:, h % 2, :], ident[:, :], start=True, stop=True)
                    pe.matmul(mix_ps[0:D, 0, P:2 * P], q_w[:, h * D:(h + 1) * D], xa[:, :],
                              start=True, stop=True).then_inc(kq_ready, 1)

                def head_scores(h):
                    pe.wait_ge(kq_copied, (g - 1) * H + h + 1)
                    scores(qT[:, h % 2, :], KT[:, h, :], (N - P) - place * P)

                keys_and_queries(0)
                pe.wait_ge(proj_taken, g)
                head_scores(0)
                for h in range(H):
                    if h + 1 < H:
                        keys_and_queries(h + 1)
                    flip_probs(base + h)
                    if h + 1 < H:
                        head_scores(h + 1)
                    weigh(base + h, lambda j: VV[:, j, h, :])
                pe.wait_ge(heads_ready, g)
                for c in range(H // 2):
                    last = pe.transpose(ring[:, 0, c * P:(c + 1) * P],
                                        o_all[:, 2 * c:2 * c + 2, :].rearrange("p a d -> p (a d)"), ident[:, :])
                last.then_inc(headsT_ready, 1)
                pe.wait_ge(headsT_copied, g)
                for c in range(H // 2):
                    last = pe.matmul(ring[:, 1, 0:D], oT_all[:, c, :], o_w[:, c, :], start=(c == 0), stop=(c == H // 2 - 1))
                last.then_inc(proj_ready, 1)


            def F(b, piece, done, base):
                pe.wait_ge(proj_taken, done + 1)
                if piece == 0:
                    pe.wait_ge(rows_ready, b * 2 + 1)
                    flip_rows(pe, ring[:, 0:2, :].rearrange("p a c -> p (a c)"), x3, ident).then_inc(l1_ready, 1)
                    for which, bank in ((1, 2), (0, 0)):
                        pe.wait_ge(l1_copied, b * 4 + (2 - which))
                        for half in range(2):
                            last = pe.matmul(ring[:, bank + half, :], l1_w[:, which, :],
                                             xT[0:D, half * HALF_N:(half + 1) * HALF_N], start=True, stop=True)
                        last.then_inc(l1_ready, 1)
                    pe.wait_ge(l1_copied, b * 4 + 3)
                if piece in (1, 2):
                    first = (piece - 1) * NB // 2
                    for i in range(NB // 2):
                        at = (first + i) * P
                        if i == 0:
                            scores(qT1[:, at:at + P], kT1)
                        flip_probs(base + i)
                        if i + 1 < NB // 2:
                            scores(qT1[:, at + P:at + 2 * P], kT1)
                        weigh(base + i, lambda j: x3[:, j, :])
                if piece == 3:
                    pe.wait_ge(rows_ready, b * 2 + 2)
                    flip_rows(pe, ring[:, 0:2, :].rearrange("p a c -> p (a c)"), x4, ident).then_inc(l1_ready, 1)
                    pe.wait_ge(l1_copied, b * 4 + 4)
                    for t in range(NB):
                        last = pe.matmul(mix_ps[:, 1, t * E:(t + 1) * E], xT[0:D, t * P:(t + 1) * P], router[:, :],
                                         start=True, stop=True)
                    last.then_inc(logits_ready, 1)
                if piece in (4, 5):
                    half = piece - 4
                    at = half * HALF_N
                    if half:
                        pe.wait_ge(y_taken, b * NB + NB // 2)
                    for e2 in range(E // 2):
                        pe.matmul(ring[:, e2, :], w1[:, e2 * P:(e2 + 1) * P], xT[:, at:at + HALF_N],
                                  start=True, stop=True).then_inc(hid_ready, 1)
                    pe.wait_ge(hid_taken, b * E + (half + 1) * E // 2)
                    for t in range(NB // 2):
                        pe.matmul(ring[:, t, :], ones[:, :], b2[:, :], start=True, stop=False, skip_group_check=True)
                        for e2 in range(E // 2):
                            last = pe.matmul(ring[:, t, e2 * P:(e2 + 1) * P], hT[e2][:, t * P:(t + 1) * P],
                                             w2[:, e2, :], start=False, stop=True, skip_group_check=True)
                        last.then_inc(y_ready, 1)

            T(0)
            T(1)
            pe.wait_ge(loaded, 16 * N_LOADS)
            pe.wait_ge(consts_set, 1)
            schedule(pe, step, F)
            step(TB, NB - 1, cores(B, TB - 1, 0), more=False)
            for piece in range(PIECES):
                F(B - 1, piece, TB, cores(B, TB, piece))

        @block.scalar
        def _(act):
            def T_queries(g):
                act.wait_ge(q_ready, g + 2)
                act.wait_ge(sim_ready, g + 1)
                act.activation(qT_pk[:, :, :], sim_ps[:, 0:H, :].rearrange("p a k -> p (a k)")
                               .rearrange("p (c t) -> p c t", c=4), ACT.Copy).then_inc(q_copied, 1)

            def T_exp(g):
                act.wait_ge(e_in_ready, g + 1)
                act.activation(e_out[:, :, :], e_in[:, :, :], ACT.Exp).then_inc(e_out_ready, 1)

            def core(n, side):
                act.wait_ge(max_ready, n + 1)
                act.activation(prob[:, :], ring[:, 0:2, :].rearrange("p a c -> p (a c)"), ACT.Exp,
                               bias=minus_max[:, side:side + 1]).then_inc(p_ready, 1)
                act.wait_ge(pT_ready, n + 1)
                act.activation(probT[:, :], ring[:, 2:4, :].rearrange("p a c -> p (a c)"), ACT.Copy)\
                   .then_inc(pT_copied, 1)

            def step(g, place, base, more=True):
                if more:
                    T_queries(g + 1)

                def copy_kq(h):
                    act.wait_ge(kq_ready, g * H + (h + 2 - H))
                    act.activation(KT[:, h, bass.ds(place * P, P)], mix_ps[0:D, 0, 0:P], ACT.Copy)
                    act.activation(qT[:, h % 2, :], mix_ps[0:D, 0, P:2 * P], ACT.Copy, scale=ATTN_SCALE)\
                       .then_inc(kq_copied, 1)

                copy_kq(0)
                for h in range(H):
                    if h + 1 < H:
                        copy_kq(h + 1)
                    core(base + h, h % 2)
                    if h == H - 2 and more:
                        T_exp(g + 1)
                act.wait_ge(headsT_ready, g)
                act.activation(oT_all[:, :, :].rearrange("p c t -> p (c t)"), ring[:, 0, :], ACT.Copy)\
                   .then_inc(headsT_copied, 1)

            def F(b, piece, done, base):
                if piece in (0, 3):
                    n = piece // 3
                    act.wait_ge(ln_var, b * 2 + n + 1)
                    act.activation(stat[:, 3, :], stat[:, 0, :], ACT.Sqrt).then_inc(ln_std, 1)
                    act.wait_ge(l1_ready, b * 4 + (1, 4)[n])
                    act.activation(xT[0:D, :], ring[0:D, 0:2, :].rearrange("p a c -> p (a c)"), ACT.Copy)\
                       .then_inc(l1_copied, 1)
                if piece == 0:
                    act.wait_ge(l1_ready, b * 4 + 2)
                    act.activation(kT1[:, :], ring[0:D, 2:4, :].rearrange("p a c -> p (a c)"), ACT.Copy)\
                       .then_inc(l1_copied, 1)
                    act.wait_ge(l1_ready, b * 4 + 3)
                    act.activation(qT1[:, :], ring[0:D, 0:2, :].rearrange("p a c -> p (a c)"), ACT.Copy,
                                   scale=ATTN_SCALE).then_inc(l1_copied, 1)
                if piece in (1, 2):
                    for i in range(NB // 2):
                        core(base + i, i % 2)
                if piece == 3:
                    act.wait_ge(route_in, b + 1)
                    act.activation(pr[:, :, :], lg[:, :, :], ACT.Exp).then_inc(route_out, 1)
                if piece in (4, 5):
                    for e2 in range(E // 2):
                        act.wait_ge(hid_ready, b * E + (piece - 4) * E // 2 + e2 + 1)
                        act.activation(hT[e2], ring[:, e2, :], ACT.Gelu).then_inc(hid_taken, 1)

            T_queries(0)
            T_exp(0)
            T_queries(1)
            T_exp(1)
            schedule(act, step, F)
            step(TB, NB - 1, cores(B, TB - 1, 0), more=False)
            for piece in range(PIECES):
                F(B - 1, piece, TB, cores(B, TB, piece))

        @block.vector
        def _(dve):
            chain = Chain(dve, dve_steps)
            dve.wait_ge(T_loaded, 16 * T_LOADS)
            chain.link(dve.tensor_copy(rank_h[:, :], rank[:, :]))

            def best_places(values, again, found, where, js):
                for j in js:
                    chain.mark(dve.max_index(where[:, j, 0:8], found[:, j, 0:8], values[:, j, :]))
                    chain.mark(dve.match_replace(again[:, j, :], found[:, j, 0:8], values[:, j, :], LOWEST))
                chain.wait()

            def one_hot(heads, free):
                for h in heads:
                    chain.link(dve.tensor_tensor(hot, bc(FIf[:, h, :], 2, CAND), bc(rank_h[:, :], 1, TOPK), ALU.is_equal))
                    chain.link(dve.tensor_tensor(hot, hot, bc(CI[:, h, :], 1, TOPK), ALU.mult))
                    chain.link(dve.tensor_reduce(row[:, h, :], hot, AX, ALU.add))
                h = slice(heads[0], heads[-1] + 1)
                chain.link(dve.tensor_tensor(next_i[:, h, :], row[:, h, :], head_base[:, h, :], ALU.add))
                if free:
                    chain.link(dve.tensor_copy(slot_i[:, h, :], next_i[:, h, :]))
                    dve.sem_inc(slot_ready, len(heads))

            T_PARTS = 10

            def T(g, part, free=False):
                if part == 0:
                    dve.wait_ge(sim_ready, g + 2)
                    chain.link(dve.tensor_copy(S[:, :, :], sim_ps[:, :, :]))
                    dve.sem_inc(sim_taken, 1)
                    for j in range(2 * H):
                        chain.mark(dve.max(V[:, j, 0:8], S[:, j, :]))
                    chain.wait()
                if part in (1, 2):
                    best_places(S, S2, V, I, range((part - 1) * H, part * H))
                if part == 3:
                    for j in range(2 * H):
                        chain.mark(dve.max(V[:, j, 8:16], S2[:, j, :]))
                    chain.wait()
                if part == 4:
                    for j in range(2 * H):
                        chain.mark(dve.max_index(I[:, j, 8:16], V[:, j, 8:16], S2[:, j, :]))
                    chain.wait()
                if part == 5:
                    chain.link(dve.tensor_copy(If[:, :, :], I[:, :, :]))
                    chain.link(dve.tensor_scalar(If[:, H:2 * H, :], If[:, H:2 * H, :], float(NK), -float(NK * NK // 2),
                                                 ALU.mult, ALU.add))
                    at = 0
                    for a0, na, nb in RECTS:
                        for dst, src in ((C, V), (CI, If)):
                            chain.mark(dve.tensor_tensor(
                                dst[:, :, at:at + na * nb].rearrange("p h (x y) -> p h x y", y=nb),
                                bc(src[:, 0:H, a0:a0 + na], 3, nb), bc(src[:, H:2 * H, 0:nb], 2, na), ALU.add))
                        at += na * nb
                    chain.wait()
                    for h in range(H):
                        chain.mark(dve.max(FV[:, h, 0:8], C[:, h, :]))
                    chain.wait()
                if part == 6:
                    best_places(C, C2, FV, FI, range(H))
                    for h in range(H):
                        chain.mark(dve.max(FV[:, h, 8:16], C2[:, h, :]))
                    chain.wait()
                if part == 7:
                    chain.mark(dve.tensor_tensor(e_in[:, :, :], FV[:, :, :],
                                                 FV[:, :, 0:1].broadcast_to([P, H, TOPK]), ALU.subtract))
                    for h in range(H):
                        chain.mark(dve.max_index(FI[:, h, 8:16], FV[:, h, 8:16], C2[:, h, :]))
                    chain.wait()
                    dve.sem_inc(e_in_ready, 1)
                    chain.link(dve.tensor_copy(FIf[:, :, :], FI[:, :, :]))
                    one_hot(range(0, 2), free)
                if part == 8:
                    one_hot(range(2, 4), free)
                    one_hot(range(4, 6), free)
                if part == 9:
                    one_hot(range(6, 8), free)
                    dve.wait_ge(e_out_ready, g + 1)
                    chain.link(dve.tensor_reduce(e_sum[:, 0, :], e_out[:, :, :], AX, ALU.add))
                    chain.link(dve.reciprocal(e_sum[:, 1, :], e_sum[:, 0, :]))
                    chain.link(dve.tensor_tensor(next_w[:, :, :], e_out[:, :, :], bc(e_sum[:, 1, :], 2, TOPK), ALU.mult))

            def install(h):
                chain.mark(dve.tensor_copy(slot_w[:, h, :], next_w[:, h, :]))
                chain.link(dve.tensor_copy(slot_i[:, h, :], next_i[:, h, :]))
                dve.sem_inc(slot_ready, 1)

            def combine(g, place, h):
                dve.wait_ge(gathered[h], g * (16 * TOPK))
                chain.link(dve.tensor_tensor(G[:, h, :, :], G[:, h, :, :], bc(slot_w[:, h, :], 2, 2 * D), ALU.mult))
                by_dim = G[:, h, :, :].rearrange("p r d -> p d r")
                chain.mark(dve.tensor_reduce(k_new[:, h % 2, :], by_dim[:, 0:D, :], AX, ALU.add))
                chain.link(dve.tensor_reduce(VV[:, bass.ds(place, 1), h, 0:D].rearrange("p o d -> p (o d)"),
                                             by_dim[:, D:2 * D, :], AX, ALU.add))
                dve.sem_inc(kv_ready, 1)

            def maxima(n, side):
                dve.wait_ge(s_ready, n + 1)
                chain.link(dve.tensor_reduce(row_max[:, side:side + 1],
                                             ring[:, 0:2, :].rearrange("p a c -> p (a c)"), AX, ALU.max))
                dve.tensor_scalar(minus_max[:, side:side + 1], row_max[:, side:side + 1], -1.0, None, ALU.mult)\
                   .then_inc(max_ready, 1)

            def output(n, side, dst, add=None):
                o = mix_ps[:, 1, 0:D]
                dve.wait_ge(o_ready, n + 1)
                chain.link(dve.reciprocal(rz[:, side:side + 1], mix_ps[:, 1, D:D + 1]))
                if add is None:
                    chain.link(dve.tensor_scalar(dst, o, rz[:, side:side + 1], None, ALU.mult))
                else:
                    chain.link(dve.scalar_tensor_tensor(dst, o, rz[:, side:side + 1], add, ALU.mult, ALU.add))
                dve.sem_inc(o_taken, 1)

            def step(g, place, base, more=True):
                for h in range(T_PARTS):
                    if h < H:
                        combine(g, place, h)
                        if more:
                            install(h)
                    if 1 <= h <= H:
                        maxima(base + (h - 1), (h - 1) % 2)
                    if h >= 2:
                        output(base + (h - 2), h % 2, o_all[:, h - 2, :])
                    if more:
                        T(g + 1, h)
                dve.sem_inc(heads_ready, 1)
                hg = st["h"][:, bass.ds(g - 1, 1), :].rearrange("p o d -> p (o d)")
                dve.wait_ge(proj_ready, g)
                chain.link(dve.tensor_tensor(hg, ring[:, 1, 0:D], hg, ALU.add))
                dve.sem_inc(proj_taken, 1)
                chain.clear()

            def norm(b, n, dst):
                layernorm_a(dve, chain, st["h"][:, bass.ds(b * NB, NB), :], xc[:, :, :], sq[:, :, :], stat)
                dve.tensor_copy(stat[:, 0, :], stat[:, 2, :]).then_inc(ln_var, 1)
                dve.wait_ge(ln_std, b * 2 + n + 1)
                chain.link(dve.reciprocal(stat[:, 1, :], stat[:, 3, :]))
                chain.link(dve.tensor_tensor(dst, xc[:, :, :], bc(stat[:, 1, :], 2, D), ALU.mult))
                dve.sem_inc(rows_ready, 1)

            def F(b, piece, done, base):
                if piece == 0:
                    norm(b, 0, x3[:, :, 0:D])
                if piece in (1, 2):
                    first = (piece - 1) * NB // 2
                    maxima(base, 0)
                    for i in range(NB // 2):
                        if i + 1 < NB // 2:
                            maxima(base + (i + 1), (i + 1) % 2)
                        hi = st["h"][:, bass.ds(b * NB + (first + i), 1), :].rearrange("p o d -> p (o d)")
                        output(base + i, i % 2, hi, add=hi)
                if piece == 3:
                    norm(b, 1, x4[:, :, :])
                    dve.wait_ge(logits_ready, b + 1)
                    chain.link(dve.tensor_copy(gate[:, :, :], mix_ps[:, 1, 0:NB * E].rearrange("p (t e) -> p t e", e=E)))
                    chain.link(dve.tensor_reduce(r8[:, 0, :], gate[:, :, :], AX, ALU.max))
                    dve.tensor_tensor(lg[:, :, :], gate[:, :, :], bc(r8[:, 0, :], 2, E), ALU.subtract)\
                       .then_inc(route_in, 1)
                    dve.wait_ge(route_out, b + 1)
                    chain.link(dve.tensor_reduce(r8[:, 1, :], pr[:, :, :], AX, ALU.add))
                    chain.link(dve.reciprocal(r8[:, 0, :], r8[:, 1, :]))
                    chain.link(dve.tensor_tensor(gate[:, :, :], pr[:, :, :], bc(r8[:, 0, :], 2, E), ALU.mult))
                    for t in range(NB):
                        chain.mark(dve.max(pv[:, t, :], gate[:, t, :]))
                    chain.wait()
                    for t in range(NB):
                        chain.mark(dve.max_index(pi[:, t, :], pv[:, t, :], gate[:, t, :]))
                    chain.wait()
                    chain.mark(dve.tensor_copy(pif[:, :, :], pi[:, :, :]))
                    chain.link(dve.tensor_tensor(r8[:, 0, :], pv[:, :, 0], pv[:, :, 1], ALU.add))
                    chain.link(dve.tensor_scalar(r8[:, 0, :], r8[:, 0, :], 1e-12, None, ALU.max))
                    chain.link(dve.reciprocal(r8[:, 1, :], r8[:, 0, :]))
                    for k in range(2):
                        chain.link(dve.tensor_tensor(comb[:, k], bc(expert_id[:, :], 1, NB),
                                                     pif[:, :, k:k + 1].broadcast_to([P, NB, E]), ALU.is_equal))
                        chain.link(dve.tensor_tensor(comb[:, k], comb[:, k],
                                                     pv[:, :, k:k + 1].broadcast_to([P, NB, E]), ALU.mult))
                    chain.link(dve.tensor_tensor(comb[:, 0], comb[:, 0], comb[:, 1], ALU.add))
                    chain.link(dve.tensor_tensor(gate[:, :, :], comb[:, 0], bc(r8[:, 1, :], 2, E), ALU.mult))
                if piece in (4, 5):
                    for t in range(NB // 2):
                        at = (piece - 4) * NB // 2 + t
                        dve.wait_ge(y_ready, b * NB + (at + 1))
                        chain.link(dve.tensor_tensor(yw[:, :, :], ring[:, t, :].rearrange("p (e d) -> p e d", e=E),
                                                     bc(gate[:, at, :], 2, D), ALU.mult))
                        dve.sem_inc(y_taken, 1)
                        chain.link(dve.tensor_reduce(sq[:, at, :], yw[:, :, :].rearrange("p e d -> p d e"), AX, ALU.add))
                if piece == 5:
                    chain.link(dve.tensor_tensor(sq[:, :, :], sq[:, :, :], x4[:, :, :], ALU.add))
                    dve.wait_ge(out_stored, b * 16 + 1)
                    chain.link(dve.tensor_tensor(out_sb[:, :, :], sq[:, :, :], st["h"][:, bass.ds(b * NB, NB), :], ALU.add))
                    dve.sem_inc(out_ready, 1)
                chain.clear()

            for part in range(T_PARTS):
                if part == 7:
                    dve.wait_ge(loaded, 16 * N_LOADS)
                    chain.link(dve.tensor_copy(causal[:, :], G[:, 0, 0:2 * NB - 1, :].rearrange("p r d -> p (r d)")))
                T(0, part, free=True)
            chain.mark(dve.tensor_copy(slot_w[:, :, :], next_w[:, :, :]))
            chain.mark(dve.tensor_copy(ident_b[:, :], ident[:, :]))
            chain.mark(dve.memset(KT[:, :, :], 0.0))
            chain.mark(dve.memset(VV[:, :, :, 0:D], 0.0))
            chain.mark(dve.memset(VV[:, :, :, D:D + 1], 1.0))
            chain.mark(dve.memset(x3[:, :, D:D + 1], 1.0))
            chain.mark(dve.memset(xT[D:D + 1, :], 1.0))
            chain.link(dve.memset(ones[:, :], 1.0))
            dve.sem_inc(consts_set, 1)
            for part in range(T_PARTS):
                T(1, part)
            chain.clear()
            schedule(dve, step, F)
            step(TB, NB - 1, cores(B, TB - 1, 0), more=False)
            for piece in range(PIECES):
                F(B - 1, piece, TB, cores(B, TB, piece))


def tower(nc, a, out, stages=99, probe=None):
    with ExitStack() as ctx:
        m = Mem(nc, ctx, "st")
        st = {
            "h": m.sb("h", [P, TB, D]),
            "xnT_d": nc.dram_tensor("xnT_scratch", (D, T + P), F32).ap(),
        }
        with ExitStack() as toeplitz:
            mt = Mem(nc, toeplitz, "tz")
            st["xnT"] = mt.sb("xnT", [D, T])
            st["u"] = mt.sb("u", [P, TB, D1])
            st["xn"] = mt.sb("xn", [P, TB, D])
            st["v"] = mt.sb("v", [P, NB, B, D1])
            st["y"] = mt.sb("y", [P, NB, B * D1])
            st["rpe"] = mt.sb("rpe", [P, NB, 2, RPE])
            embed_stage(nc, a, st)
            if stages == 1: return probe(nc, m, st)
            conv_stage(nc, a, st)
            if stages == 2: return probe(nc, m, st)
            gate_stage(nc, a, st)
            if stages == 3: return probe(nc, m, st)
        mixer_stage(nc, a, st, out)


def data_layout(inputs):
    f = {k: np.ascontiguousarray(v) for k, v in inputs.items()}
    row = lambda *v: np.concatenate([f[n].reshape(-1) for n in v])[None, :]
    A = "L0_attn_"
    keys = np.zeros((4, DK, 4, 4, NK), np.float32)
    for c in range(4):
        for i in range(4):
            keys[i, :, c, i, :] = f["L0_ffn_pk_keys"][c // 2, :, 4 * (c % 2) + i, :].T
    l1_w = np.zeros((D, 2, P), np.float32)
    l1_w[:, 0, :D], l1_w[:, 1, :D] = f["L1_attn_Wq"].T, f["L1_attn_Wk"].T
    w2 = np.zeros((2, D, E // 2, 2, D), np.float32)
    for e in range(E):
        w2[e % 2, :, e // 2, e % 2, :] = f["L1_ffn_w2"][e]
    d = {
        "ids": np.ascontiguousarray(f["x"].reshape(TB, P).T),
        "tok_W": np.ascontiguousarray(f["L0_tok_W"].T),
        "uv_w": np.concatenate([np.concatenate([f[A + "u_w"].T, f[A + "v_w"].T], 1), row(A + "u_b", A + "v_b")], 0),
        "rpe_w": row(A + "pos_w", A + "pos_b", A + "rpe_lw", A + "rpe_lb"),
        "kernel_w": np.concatenate([f[A + "out_w"].T, f[A + "out_w"].T, row(A + "out_b")], 0),
        "o_w": np.concatenate([f[A + "o_w"].T, row(A + "o_b")], 0),
        "pk_w": f["L0_ffn_Wq_pk"],
        "pk_keys": keys.reshape(P, 4 * 4 * NK),
        "kv_table": np.concatenate([f["L0_ffn_keys_table"], f["L0_ffn_values_table"]], 1),
        "q_w": f["L0_ffn_Wq"],
        "out_proj": f["L0_ffn_Wo"],
        "l1_w": l1_w.reshape(D, 2 * P),
        "router_w": f["L1_ffn_router_w"].T,
        "w1": np.concatenate([f["L1_ffn_w1"].transpose(1, 0, 2).reshape(D, E * D), row("L1_ffn_b1")], 0),
        "w2": w2.reshape(P, E // 2 * P),
        "b2": row("L1_ffn_b2"),
        "t_w": np.concatenate([f[A + "t_w"].T, row(A + "t_b")], 0),
    }
    return {k: np.ascontiguousarray(v) for k, v in d.items()}


def kernel(**inputs):
    import concourse.bacc as bacc
    from concourse.bass_utils import run_bass_kernel_spmd

    nc = bacc.Bacc("TRN2", target_bir_lowering=False, num_devices=1)
    arrays = {**data_layout({k: np.asarray(v) for k, v in inputs.items()}), **tower_constants()}
    handles = {k: nc.dram_tensor(f"in_{k}", v.shape, mybir.dt.from_np(v.dtype), kind="ExternalInput").ap()
               for k, v in arrays.items()}
    out = nc.dram_tensor("out_h", (T, D), F32, kind="ExternalOutput").ap()
    tower(nc, handles, out)
    result = run_bass_kernel_spmd(nc, [{f"in_{k}": v for k, v in arrays.items()}], core_ids=[0])
    return result.results[0]["out_h"].reshape(B, N, D)
```
